# Optimizing a Trainium2 kernel written in Bass

```python
import numpy as np
import jax
import jax.numpy as jnp

def _softmax(x, axis=-1):
    return jax.nn.softmax(x, axis=axis)

def _gelu(x):
    return jax.nn.gelu(x, approximate=True)

def _silu(x):
    return jax.nn.silu(x)

def _sigmoid(x):
    return jax.nn.sigmoid(x)

def _layernorm(x, axis=-1, eps=1e-05):
    m = jnp.mean(x, axis=axis, keepdims=True)
    v = jnp.var(x, axis=axis, keepdims=True)
    return (x - m) / jnp.sqrt(v + eps)

def _scatter_add(tgt, idx, src, axis=0):
    return tgt.at[idx].add(src)

def _segment_sum(src, seg, n):
    return jax.ops.segment_sum(src, seg, n)
kernel_name = 'mk_gnn_preln_d4_gnn_r32_597893'

def setup_inputs(seed: int=0):
    np.random.seed(seed)
    _w = jnp.asarray

    def _rec_inputs():
        import jax
        import jax.numpy as jnp
        _gk = jax.random.key(seed)
        x = -0.0005121 + 1.001 * jax.random.normal(jax.random.fold_in(_gk, 1), (3125, 64), jnp.float32)
        _s = jax.random.randint(jax.random.fold_in(_gk, 2), (50000,), 0, 3125, jnp.int32)
        _d = jax.random.randint(jax.random.fold_in(_gk, 3), (50000,), 0, 3125, jnp.int32)
        _loop = jnp.arange(3125, dtype=jnp.int32)
        src = jnp.concatenate([_s, _d, _loop])
        dst = jnp.concatenate([_d, _s, _loop])
        _o = jnp.argsort(dst, stable=True)
        src = src[_o]
        dst = dst[_o]
        edge_attr_8 = -0.000153872 + 1.00011 * jax.random.normal(jax.random.fold_in(_gk, 12), (103125, 8), jnp.float32)
        edge_type_8 = jax.random.randint(jax.random.fold_in(_gk, 14), (103125,), 0, 8, jnp.int32)
        edge_weight = jax.random.uniform(jax.random.fold_in(_gk, 15), (103125,), jnp.float32, 0.0, 1)
        return (x, src, dst, edge_attr_8, edge_type_8, edge_weight)
    x, src, dst, edge_attr_8, edge_type_8, edge_weight = _rec_inputs()

    def _L0_gnn_setup():
        import jax, jax.numpy as jnp
        import numpy as np
        NEG_SLOPE = 0.2

        def gatv2_layer(x, src, dst, Wl, Wr, att, bias, heads, out_ch):
            N = x.shape[0]
            xl = (x @ Wl).reshape(N, heads, out_ch)
            xr = (x @ Wr).reshape(N, heads, out_ch)
            m = xl[src] + xr[dst]
            e = jnp.sum(jax.nn.leaky_relu(m, NEG_SLOPE) * att, -1)
            emax = jax.ops.segment_max(e, dst, num_segments=N)
            ee = jnp.exp(e - emax[dst])
            denom = jax.ops.segment_sum(ee, dst, num_segments=N)
            alpha = ee / denom[dst]
            out = jax.ops.segment_sum(alpha[..., None] * xl[src], dst, num_segments=N)
            return out.reshape(N, heads * out_ch) + bias
        key = jax.random.key(seed)
        ks = jax.random.split(key, 10)
        N, E, F_in, hid, out_ch, H = (50000, 25000, 64, 64, 64, 4)
        x = jax.random.normal(ks[0], (N, F_in), dtype=jnp.float32)
        edge_index = jax.random.randint(ks[1], (2, E), 0, N, dtype=jnp.int64)
        s1 = 1.0 / np.sqrt(F_in)
        Wl1 = jax.random.normal(ks[2], (F_in, H * hid), dtype=jnp.float32) * s1
        Wr1 = jax.random.normal(ks[3], (F_in, H * hid), dtype=jnp.float32) * s1
        att1 = jax.random.normal(ks[4], (H, hid), dtype=jnp.float32) * (1.0 / np.sqrt(hid))
        b1 = jnp.zeros((H * hid,), dtype=jnp.float32)
        s2 = 1.0 / np.sqrt(H * hid)
        Wl2 = jax.random.normal(ks[5], (H * hid, out_ch), dtype=jnp.float32) * s2
        Wr2 = jax.random.normal(ks[6], (H * hid, out_ch), dtype=jnp.float32) * s2
        att2 = jax.random.normal(ks[7], (1, out_ch), dtype=jnp.float32) * (1.0 / np.sqrt(out_ch))
        b2 = jnp.zeros((out_ch,), dtype=jnp.float32)
        return {'x': x, 'Wl1': Wl1, 'Wr1': Wr1, 'att1': att1, 'b1': b1, 'Wl2': Wl2, 'Wr2': Wr2, 'att2': att2, 'b2': b2, 'edge_index': edge_index}
    _L0_gnn_all = _L0_gnn_setup()
    _L0_gnn_in = {k: v for k, v in _L0_gnn_all.items() if k in ('Wl1', 'Wr1', 'att1', 'b1', 'Wl2', 'Wr2', 'att2', 'b2')}
    del _L0_gnn_all

    def _L1_gnn_setup():
        import jax, jax.numpy as jnp
        import numpy as np
        N_NODES = 50000
        N_EDGES = 25000
        F = 64
        N_ETYPES = 8
        key = jax.random.key(seed)
        ks = jax.random.split(key, 8)
        nfeat = jax.random.normal(ks[0], (N_NODES, F), dtype=jnp.float32)
        src = jax.random.randint(ks[1], (N_EDGES,), 0, N_NODES)
        dst = jax.random.randint(ks[2], (N_EDGES,), 0, N_NODES)
        etype = jax.random.randint(ks[3], (N_EDGES,), 0, N_ETYPES)
        scale = 1.0 / np.sqrt(F)
        head_w = jax.random.normal(ks[4], (F,), dtype=jnp.float32) * scale
        tail_w = jax.random.normal(ks[5], (F,), dtype=jnp.float32) * scale
        head_b = jnp.zeros((1,), dtype=jnp.float32)
        tail_b = jnp.zeros((1,), dtype=jnp.float32)
        rel_w = jax.random.normal(ks[6], (N_ETYPES,), dtype=jnp.float32) * scale
        return {'nfeat': nfeat, 'src': src, 'dst': dst, 'etype': etype, 'head_w': head_w, 'head_b': head_b, 'tail_w': tail_w, 'tail_b': tail_b, 'rel_w': rel_w}
    _L1_gnn_all = _L1_gnn_setup()
    _L1_gnn_in = {k: v for k, v in _L1_gnn_all.items() if k in ('head_w', 'head_b', 'tail_w', 'tail_b', 'rel_w')}
    del _L1_gnn_all

    def _L2_gnn_setup():
        import jax, jax.numpy as jnp
        import numpy as np
        NUM_LAYERS = 2
        GCN_WEIGHT = 0.5
        N_NODES = 3125
        N_EDGES = 37500
        D_FEAT = 64
        key = jax.random.key(seed)
        k1, k2, k3, k4 = jax.random.split(key, 4)
        raw_features = jax.random.normal(k1, (N_NODES, D_FEAT), dtype=jnp.float32)
        edge_weight = jax.random.uniform(k2, (N_EDGES,), dtype=jnp.float32)
        edge_src = jax.random.randint(k3, (N_EDGES,), 0, N_NODES, dtype=jnp.int32)
        edge_dst = jnp.sort(jax.random.randint(k4, (N_EDGES,), 0, N_NODES, dtype=jnp.int32))
        return {'raw_features': raw_features, 'edge_weight': edge_weight, 'edge_src': edge_src, 'edge_dst': edge_dst}
    _L2_gnn_all = _L2_gnn_setup()
    _L2_gnn_in = {k: v for k, v in _L2_gnn_all.items() if k in ()}
    del _L2_gnn_all

    def _L3_gnn_setup():
        import jax, jax.numpy as jnp
        import numpy as np
        N_NODES = 625
        N_EDGES = 31250
        C = 64
        H = 64
        N_BASIS = 8
        key = jax.random.key(seed)
        ks = jax.random.split(key, 10)

        def glorot(k, shape):
            fan_in, fan_out = (shape[0], shape[1])
            lim = np.sqrt(6.0 / (fan_in + fan_out)).astype(np.float32)
            return jax.random.uniform(k, shape, jnp.float32, -lim, lim)
        return {'p': jax.random.normal(ks[0], (N_NODES, C), jnp.float32), 'idx_i': jax.random.randint(ks[1], (N_EDGES,), 0, N_NODES), 'idx_j': jax.random.randint(ks[2], (N_EDGES,), 0, N_NODES), 'basis': jax.random.normal(ks[3], (N_EDGES, N_BASIS), jnp.float32), 'pp_W': glorot(ks[4], (C, C)), 'pp_b': jnp.zeros((C,), jnp.float32), 'pi_W1': glorot(ks[5], (2 * C, H)), 'pi_b1': jnp.zeros((H,), jnp.float32), 'pi_W2': glorot(ks[6], (H, H * N_BASIS)), 'ii_W': glorot(ks[7], (H, C)), 'ii_b': jnp.zeros((C,), jnp.float32)}
    _L3_gnn_all = _L3_gnn_setup()
    _L3_gnn_in = {k: v for k, v in _L3_gnn_all.items() if k in ('pp_W', 'pp_b', 'pi_W1', 'pi_b1', 'pi_W2', 'ii_W', 'ii_b')}
    del _L3_gnn_all
    return {'x': x, 'src': src, 'dst': dst, 'edge_attr_8': edge_attr_8, 'edge_type_8': edge_type_8, 'edge_weight': edge_weight, 'L0_gnn_Wl1': _L0_gnn_in['Wl1'], 'L0_gnn_Wr1': _L0_gnn_in['Wr1'], 'L0_gnn_att1': _L0_gnn_in['att1'], 'L0_gnn_b1': _L0_gnn_in['b1'], 'L0_gnn_Wl2': _L0_gnn_in['Wl2'], 'L0_gnn_Wr2': _L0_gnn_in['Wr2'], 'L0_gnn_att2': _L0_gnn_in['att2'], 'L0_gnn_b2': _L0_gnn_in['b2'], 'L1_gnn_head_w': _L1_gnn_in['head_w'], 'L1_gnn_head_b': _L1_gnn_in['head_b'], 'L1_gnn_tail_w': _L1_gnn_in['tail_w'], 'L1_gnn_tail_b': _L1_gnn_in['tail_b'], 'L1_gnn_rel_w': _L1_gnn_in['rel_w'], 'L3_gnn_pp_W': _L3_gnn_in['pp_W'], 'L3_gnn_pp_b': _L3_gnn_in['pp_b'], 'L3_gnn_pi_W1': _L3_gnn_in['pi_W1'], 'L3_gnn_pi_b1': _L3_gnn_in['pi_b1'], 'L3_gnn_pi_W2': _L3_gnn_in['pi_W2'], 'L3_gnn_ii_W': _L3_gnn_in['ii_W'], 'L3_gnn_ii_b': _L3_gnn_in['ii_b']}

def reference(x, src, dst, edge_attr_8, edge_type_8, edge_weight, L0_gnn_Wl1, L0_gnn_Wr1, L0_gnn_att1, L0_gnn_b1, L0_gnn_Wl2, L0_gnn_Wr2, L0_gnn_att2, L0_gnn_b2, L1_gnn_head_w, L1_gnn_head_b, L1_gnn_tail_w, L1_gnn_tail_b, L1_gnn_rel_w, L3_gnn_pp_W, L3_gnn_pp_b, L3_gnn_pi_W1, L3_gnn_pi_b1, L3_gnn_pi_W2, L3_gnn_ii_W, L3_gnn_ii_b):
    import jax
    import jax.numpy as jnp

    def _L0_gnn_ref(x, Wl1, Wr1, att1, b1, Wl2, Wr2, att2, b2, edge_index):
        import jax, jax.numpy as jnp
        import numpy as np
        NEG_SLOPE = 0.2

        def gatv2_layer(x, src, dst, Wl, Wr, att, bias, heads, out_ch):
            N = x.shape[0]
            xl = (x @ Wl).reshape(N, heads, out_ch)
            xr = (x @ Wr).reshape(N, heads, out_ch)
            m = xl[src] + xr[dst]
            e = jnp.sum(jax.nn.leaky_relu(m, NEG_SLOPE) * att, -1)
            emax = jax.ops.segment_max(e, dst, num_segments=N)
            ee = jnp.exp(e - emax[dst])
            denom = jax.ops.segment_sum(ee, dst, num_segments=N)
            alpha = ee / denom[dst]
            out = jax.ops.segment_sum(alpha[..., None] * xl[src], dst, num_segments=N)
            return out.reshape(N, heads * out_ch) + bias
        N = x.shape[0]
        loops = jnp.arange(N, dtype=edge_index.dtype)
        src = jnp.concatenate([edge_index[0], loops])
        dst = jnp.concatenate([edge_index[1], loops])
        h = gatv2_layer(x, src, dst, Wl1, Wr1, att1, b1, heads=4, out_ch=64)
        h = jax.nn.gelu(h, approximate=False)
        out = gatv2_layer(h, src, dst, Wl2, Wr2, att2, b2, heads=1, out_ch=64)
        return out

    def _L1_gnn_ref(nfeat, src, dst, etype, head_w, head_b, tail_w, tail_b, rel_w):
        import jax, jax.numpy as jnp
        import numpy as np
        N_NODES = 50000
        N_EDGES = 25000
        F = 64
        N_ETYPES = 8
        n = nfeat.shape[0]
        el = nfeat @ head_w + head_b[0]
        er = nfeat @ tail_w + tail_b[0]
        e = el[src] + er[dst] + rel_w[etype]
        e_max = jax.ops.segment_max(e, dst, num_segments=n)
        e_exp = jnp.exp(e - e_max[dst])
        denom = jax.ops.segment_sum(e_exp, dst, num_segments=n)
        a = e_exp / denom[dst]
        out = jax.ops.segment_sum(a[:, None] * nfeat[src], dst, num_segments=n)
        return out

    def _L2_gnn_ref(raw_features, edge_weight, edge_src, edge_dst):
        import jax, jax.numpy as jnp
        import numpy as np
        NUM_LAYERS = 2
        GCN_WEIGHT = 0.5
        N_NODES = 3125
        N_EDGES = 37500
        D_FEAT = 64
        n = raw_features.shape[0]
        deg = jax.ops.segment_sum(jnp.ones(edge_dst.shape, jnp.float32), edge_dst, num_segments=n)
        has_neigh = (deg > 0)[:, None]
        h = raw_features
        for _ in range(NUM_LAYERS):
            msgs = h[edge_src] * edge_weight[:, None]
            agg = jax.ops.segment_sum(msgs, edge_dst, num_segments=n)
            agg = jnp.where(has_neigh, agg, h)
            h = h * GCN_WEIGHT + agg * (1.0 - GCN_WEIGHT)
        return h

    def _L3_gnn_ref(p, idx_i, idx_j, basis, pp_W, pp_b, pi_W1, pi_b1, pi_W2, ii_W, ii_b):
        import jax, jax.numpy as jnp
        import numpy as np
        N_NODES = 625
        N_EDGES = 31250
        C = 64
        H = 64
        N_BASIS = 8
        p1 = jnp.tanh(p @ pp_W + pp_b)
        pair = jnp.concatenate([p1[idx_i], p1[idx_j]], axis=-1)
        h = pair @ pi_W1 + pi_b1
        h = (h @ pi_W2).reshape(-1, H, N_BASIS)
        i1 = jnp.einsum('ecb,eb->ec', h, basis)
        i2 = jnp.tanh(i1 @ ii_W + ii_b)
        return p.at[idx_i].add(i2)
    edge_index = jnp.stack([src, dst])
    h = jnp.maximum(_layernorm(x, axis=-1), 0.0)
    x = x + _L0_gnn_ref(h, L0_gnn_Wl1, L0_gnn_Wr1, L0_gnn_att1, L0_gnn_b1, L0_gnn_Wl2, L0_gnn_Wr2, L0_gnn_att2, L0_gnn_b2, edge_index)
    h = jnp.maximum(_layernorm(x, axis=-1), 0.0)
    x = x + _L1_gnn_ref(h, src, dst, edge_type_8, L1_gnn_head_w, L1_gnn_head_b, L1_gnn_tail_w, L1_gnn_tail_b, L1_gnn_rel_w)
    h = jnp.maximum(_layernorm(x, axis=-1), 0.0)
    x = x + _L2_gnn_ref(h, edge_weight, src, dst)
    h = jnp.maximum(_layernorm(x, axis=-1), 0.0)
    x = x + _L3_gnn_ref(h, src, dst, edge_attr_8, L3_gnn_pp_W, L3_gnn_pp_b, L3_gnn_pi_W1, L3_gnn_pi_b1, L3_gnn_pi_W2, L3_gnn_ii_W, L3_gnn_ii_b)
    return x

_drawn_inputs = setup_inputs


def setup_inputs(seed=0):
    import zlib

    import numpy as np

    out = dict(_drawn_inputs(seed))
    spreads = {'L0_gnn_b1': (0.0, 0.1),
     'L0_gnn_b2': (0.0, 0.1),
     'L3_gnn_pp_b': (0.0, 0.518),
     'L3_gnn_pi_b1': (0.0, 0.472),
     'L3_gnn_ii_b': (0.0, 0.1)}
    factors = {'L0_gnn_Wr1': 36.176,
     'L0_gnn_Wr2': 64.0,
     'L0_gnn_att2': 64.0,
     'L1_gnn_tail_w': 64.0,
     'L1_gnn_rel_w': 37.381}
    for name, (base, spread) in spreads.items():
        noise = np.random.default_rng([zlib.crc32(name.encode()), seed]).standard_normal(out[name].shape)
        drawn = base * np.exp(spread * noise) if base else spread * noise
        out[name] = jnp.asarray(drawn.astype(out[name].dtype))
    for name, factor in factors.items():
        out[name] = (out[name] * factor).astype(out[name].dtype)
    return out
```

```python
from contextlib import ExitStack

import numpy as np

import concourse.bass as bass
from concourse import mybir

F32 = mybir.dt.float32
BF16 = mybir.dt.bfloat16
I32 = mybir.dt.int32
ALU = mybir.AluOpType
ACT = mybir.ActivationFunctionType
AX_X = mybir.AxisListType.X

P = 128
N = 3125
E = 103125
D = 64
HEADS = 4
WIDE = HEADS * D
ET = 125
TILES = E // ET
BT = 11
BLOCKS = TILES // BT
BE = BT * ET
RING = 3
NT = N // ET
PADT = 2
NP = (NT + PADT) * ET
PARTS = 3
NARROW, FULL = 32, 128
BIG = 1e30
TINY = 1e-30
SLOPE = 0.2
EPS = 1e-5
NBASIS = 8
COPIES = 3
assert TILES * ET == E and BLOCKS * BT == TILES and BLOCKS % RING == 0 and NT * ET == N
assert 2 * (FULL - 1) < PADT * ET + FULL


class Stage:

    def __init__(self, nc, tag):
        self.nc, self.tag, self.ctx, self.nums = nc, tag, ExitStack(), []

    def sb(self, name, shape, dt=F32):
        return self.ctx.enter_context(self.nc.sbuf_tensor(f"{self.tag}_{name}", shape, dt))

    def bank(self, name, dt=F32):
        words = 512 if dt == F32 else 1024
        return self.ctx.enter_context(self.nc.psum_tensor(f"{self.tag}_ps_{name}", [P, words], dt))

    def sem(self, name):
        s = self.ctx.enter_context(self.nc.semaphore(f"{self.tag}_{name}"))
        self.nums.append(s.num)
        return s

    def __enter__(self):
        return self

    def __exit__(self, *e):
        if e[0] is None and self.nums:
            self.nc.all_engine_barrier(sems_to_clear=range(min(self.nums), max(self.nums) + 1))
        self.ctx.close()
        return False


class Core:

    def __init__(self, nc, ctx, a):
        self.nc, self.a = nc, a

        def sb(name, shape, dt=F32):
            return ctx.enter_context(nc.sbuf_tensor(name, shape, dt))

        self.ident = sb("ident", [P, P])
        self.identb = sb("identb", [P, P], BF16)
        self.iota_row = sb("iota_row", [P, P])
        self.iota_col = sb("iota_col", [P, 3])
        self.ones = sb("ones", [P, P])
        self.x = sb("x", [ET, NT, D])
        self.h = sb("h", [ET, NT, D])
        self.rel = sb("rel", [ET, TILES])
        self.ew = sb("ew", [ET, TILES])
        self.relw = sb("relw", [ET, TILES])
        self.first = sb("first", [1, TILES], I32)
        self.span = sb("span", [1, 1], I32)
        self.times = sb("times", [ET, TILES])
        self.has_edges = sb("has_edges", [ET, NT])
        self.w_gat1 = sb("w_gat1", [D, 2, WIDE + HEADS])
        self.att1 = sb("att1", [P, 2, HEADS])
        self.w_gat2 = sb("w_gat2", [P, 2, 2 * (D + 1)])
        self.att2 = sb("att2", [D, 1])
        self.w_rel = sb("w_rel", [D, 2])
        self.b_rel = sb("b_rel", [1, 2])
        self.b1 = sb("b1", [P, 2])
        self.b2 = sb("b2", [ET, D])
        self.head_of = sb("head_of", [HEADS, 2, P])
        self.w_pp = sb("w_pp", [D, D])
        self.b_pp = sb("b_pp", [D, 1])
        self.w_pair = sb("w_pair", [D, 2, D])
        self.b_pair = sb("b_pair", [1, D])
        self.w_basis = sb("w_basis", [D, D * NBASIS])
        self.w_stack = sb("w_stack", [P, 3, D * NBASIS], BF16)
        self.b_ii = sb("b_ii", [ET, D])

        self.sofar = 0
        self.gathered = [ctx.enter_context(nc.semaphore(f"gathered{s}")) for s in range(RING)]
        self.scattered = [ctx.enter_context(nc.semaphore(f"scattered{c}")) for c in range(COPIES)]

        def dram(name, shape, dt=F32):
            return nc.dram_tensor(name, shape, dt).ap()

        self.rel_rows = dram("rel_rows", [BLOCKS, BE], BF16)
        self.reset_rows = dram("reset_rows", [BLOCKS, BE + 1], BF16)
        self.gat1_rows = dram("gat1_rows", [N, WIDE + HEADS])
        self.gat1_win = dram("gat1_win", [NP, PARTS, WIDE + HEADS], BF16)
        self.gat2_rows = dram("gat2_rows", [N, D + 2])
        self.gat2_win = dram("gat2_win", [NP, PARTS, D + 1], BF16)
        self.att_rows = dram("att_rows", [N, D + 2])
        self.att_win = dram("att_win", [NP, PARTS, 2], BF16)
        self.gcn_rows = [dram(f"gcn_rows{i}", [N, D]) for i in range(2)]
        self.pair_rows = dram("pair_rows", [N, 4 * D], BF16)
        self.pair_win = dram("pair_win", [NP, PARTS, D * NBASIS], BF16)
        self.sums = [dram(f"sums{i}", [NP, D]) for i in range(COPIES)]


def as_row(v):
    return v.rearrange("(a n) -> a n", a=1)


def prepare(core):
    nc, a = core.nc, core.a
    with Stage(nc, "prep") as st:
        dst_t = st.sb("dst_t", [ET, TILES], I32)
        first_b = st.sb("first_b", [ET, TILES], I32)
        next_t = st.sb("next_t", [ET, TILES], I32)
        type_t = st.sb("type_t", [ET, TILES], I32)
        relw_b = st.sb("relw_b", [ET, NBASIS])
        term = st.sb("term", [ET, TILES])
        dst_n = st.sb("dst_n", [BLOCKS, BE], I32)
        prev_n = st.sb("prev_n", [BLOCKS, BE], I32)
        rel_n = st.sb("rel_n", [BLOCKS, BE], BF16)
        reset_n = st.sb("reset_n", [BLOCKS, BE + 1], BF16)
        zeros = st.sb("zeros", [ET, NT + PADT, D])
        last = st.sb("last", [1, TILES], I32)
        reach = st.sb("reach", [1, TILES])
        top = st.sb("top", [1, 1])
        loaded, zeroed, stored, prev_set, step = (
            st.sem(n) for n in ("loaded", "zeroed", "stored", "prev_set", "step"))
        loads = [
            (core.ident[:, :], a["ident"]),
            (core.iota_row[:, :], as_row(a["iota"]).to_broadcast([P, P])),
            (core.iota_col[:, :], a["iota_cols"]),
            (core.x[:, :, :], a["x"].rearrange("(t p) c -> p t c", p=ET)),
            (core.ew[:, :], a["edge_weight_t"]),
            (core.first[:, :], a["dst_t"][0:1, :]),
            (last[:, :], a["dst_t"][ET - 1:ET, :]),
            (dst_t[:, :], a["dst_t"]),
            (first_b[:, :], a["dst_t"][0:1, :].to_broadcast([ET, TILES])),
            (next_t[:, :], a["next_t"]),
            (type_t[:, :], a["edge_type_t"]),
            (relw_b[:, :], as_row(a["L1_gnn_rel_w"]).to_broadcast([ET, NBASIS])),
            (dst_n[:, :], a["dst"].rearrange("(k e) -> k e", k=BLOCKS)),
            (prev_n[1:BLOCKS, :], a["dst"][BE - 1:E - 1].rearrange("(k e) -> k e", e=BE)),
            (prev_n[0:1, 1:BE], as_row(a["dst"][0:BE - 1])),
        ]
        with nc.Block() as block:

            @block.sync
            def _(sp):
                sp.wait_ge(prev_set, 1)
                for to, of in loads:
                    sp.dma_start(to, of).then_inc(loaded, 16)

            @block.gpsimd
            def _(pool):
                pool.memset(core.ones[:, :], 1.0)
                pool.memset(zeros[:, :, :], 0.0).then_inc(zeroed, 1)

            @block.scalar
            def _(act):
                act.wait_ge(zeroed, 1)
                for s in core.sums:
                    act.dma_start(s.rearrange("(t p) c -> p t c", p=ET), zeros[:, :, :]).then_inc(stored, 16)
                act.wait_ge(step, 4)
                act.dma_start(core.rel_rows, rel_n[:, :]).then_inc(stored, 16)
                act.wait_ge(step, 6)
                act.dma_start(core.reset_rows, reset_n[:, :]).then_inc(stored, 16)
                act.wait_ge(stored, 16 * (COPIES + 2))

            @block.vector
            def _(v):
                v.memset(prev_n[0:1, 0:1], -1).then_inc(prev_set, 1)
                v.wait_ge(loaded, 16 * len(loads))
                v.tensor_copy(core.identb[:, :], core.ident[:, :]).then_inc(step, 1)
                v.tensor_tensor(core.rel[:, :], dst_t[:, :], first_b[:, :], ALU.subtract).then_inc(step, 1)
                v.memset(reset_n[:, BE:BE + 1], 0.0).then_inc(step, 1)
                dst3 = dst_n[:, :].rearrange("k (t e) -> k t e", t=BT)
                v.tensor_tensor(rel_n[:, :].rearrange("k (t e) -> k t e", t=BT), dst3,
                                dst3[:, :, 0:1].to_broadcast([BLOCKS, BT, ET]), ALU.subtract).then_inc(step, 1)
                v.tensor_tensor(reset_n[:, 0:BE], dst_n[:, :], prev_n[:, :], ALU.not_equal).then_inc(step, 1)
                v.wait_ge(step, 5)
                v.tensor_scalar(reset_n[:, 0:BE], reset_n[:, 0:BE], -BIG, None, ALU.mult).then_inc(step, 1)
                v.tensor_scalar(core.relw[:, :], type_t[:, :], 0.0, relw_b[:, 0:1], ALU.is_equal,
                                ALU.mult).then_inc(step, 1)
                for k in range(1, NBASIS):
                    v.wait_ge(step, 7 + 2 * (k - 1))
                    v.tensor_scalar(term[:, :], type_t[:, :], float(k), relw_b[:, k:k + 1], ALU.is_equal,
                                    ALU.mult).then_inc(step, 1)
                    v.wait_ge(step, 8 + 2 * (k - 1))
                    v.tensor_tensor(core.relw[:, :], core.relw[:, :], term[:, :], ALU.add).then_inc(step, 1)
                n = 7 + 2 * (NBASIS - 1)
                v.tensor_tensor(reach[:, :], last[:, :], core.first[:, :], ALU.subtract).then_inc(step, 1)
                v.wait_ge(step, n + 1)
                v.tensor_reduce(top[:, :], reach[:, :], AX_X, ALU.max).then_inc(step, 1)
                v.wait_ge(step, n + 2)
                v.tensor_copy(core.span[:, :], top[:, :]).then_inc(step, 1)
                v.tensor_tensor(core.times[:, :], dst_t[:, :], next_t[:, :], ALU.not_equal).then_inc(step, 1)
                v.wait_ge(step, n + 4)
                v.tensor_scalar(core.times[:, :], core.times[:, :], 1.0, None, ALU.add).then_inc(step, 1)
                v.wait_ge(step, n + 5)


def prepare_weights(core):
    nc, a = core.nc, core.a
    with Stage(nc, "weights") as st:
        att_raw = st.sb("att_raw", [P, 2, HEADS])
        att2_raw = st.sb("att2_raw", [D, 1])
        w_pi2 = st.sb("w_pi2", [D, D * NBASIS])
        w_ii = st.sb("w_ii", [D, D])
        turned_w = st.sb("turned_w", [P, 16, P])
        rest = st.sb("rest", [D, D * NBASIS])
        parts = st.sb("parts", [D, PARTS, D * NBASIS], BF16)
        tmp = [st.bank(f"tmp{i}") for i in range(2)]
        loaded, cleared, pe_done, taken, split, stacked = (
            st.sem(n) for n in ("loaded", "cleared", "pe_done", "taken", "split", "stacked"))
        loads = [
            (core.w_gat1[:, 0, 0:WIDE], a["L0_gnn_Wl1"]),
            (core.w_gat1[:, 1, 0:WIDE], a["L0_gnn_Wr1"]),
            (core.w_gat2[:, :, 0:D], a["L0_gnn_Wl2"].rearrange("(c p) n -> p c n", p=P)),
            (core.w_gat2[:, :, D + 1:2 * D + 1], a["L0_gnn_Wr2"].rearrange("(c p) n -> p c n", p=P)),
            (att2_raw[:, :], a["L0_gnn_att2"].rearrange("a c -> c a")),
            (core.w_rel[:, 0:1], a["L1_gnn_head_w"].rearrange("(c a) -> c a", a=1)),
            (core.w_rel[:, 1:2], a["L1_gnn_tail_w"].rearrange("(c a) -> c a", a=1)),
            (core.b_rel[:, 0:1], as_row(a["L1_gnn_head_b"])),
            (core.b_rel[:, 1:2], as_row(a["L1_gnn_tail_b"])),
            (core.b1[:, :], a["L0_gnn_b1"].rearrange("(c p) -> p c", p=P)),
            (core.b2[:, :], as_row(a["L0_gnn_b2"]).to_broadcast([ET, D])),
            (core.head_of[:, :, :], a["head_of"]),
            (core.w_pp[:, :], a["L3_gnn_pp_W"]),
            (core.b_pp[:, :], a["L3_gnn_pp_b"].rearrange("(c a) -> c a", a=1)),
            (core.w_pair[:, :, :], a["L3_gnn_pi_W1"].rearrange("(s c) n -> c s n", c=D)),
            (core.b_pair[:, :], as_row(a["L3_gnn_pi_b1"])),
            (w_pi2[:, :], a["L3_gnn_pi_W2"]),
            (w_ii[:, :], a["L3_gnn_ii_W"]),
            (core.b_ii[:, :], as_row(a["L3_gnn_ii_b"]).to_broadcast([ET, D])),
        ]
        loads += [(att_raw[(h % 2) * D:(h % 2 + 1) * D, h // 2, h:h + 1],
                   a["L0_gnn_att1"][h:h + 1, :].rearrange("a c -> c a")) for h in range(HEADS)]
        pi2 = w_pi2[:, :].rearrange("k (c b) -> k b c", b=NBASIS)
        turns = []
        for side in range(2):
            for c in range(2):
                turns.append((core.w_gat1[:, side, c * P:(c + 1) * P], D, P))
        for side in range(2):
            for c in range(2):
                turns.append((core.w_gat2[:, c, side * (D + 1):side * (D + 1) + D], P, D))
        for b in range(NBASIS):
            turns.append((pi2[:, b, :], D, D))
        products = []
        for side in range(2):
            pairs = [(turned_w[:, 2 * side + c, 0:D], att_raw[:, c, :]) for c in range(2)]
            products.append((pairs, D, HEADS, core.w_gat1[:, side, WIDE:WIDE + HEADS], SLOPE))
        for side in range(2):
            for c in range(2):
                col = side * (D + 1) + D
                products.append(([(turned_w[0:D, 4 + 2 * side + c, :], att2_raw[:, :])], P, 1,
                                 core.w_gat2[:, c, col:col + 1], SLOPE))
        basis = core.w_basis[:, :].rearrange("k (c b) -> k b c", b=NBASIS)
        for b in range(NBASIS):
            products.append(([(turned_w[0:D, 8 + b, 0:D], w_ii[:, :])], D, D, basis[:, b, :], 1.0))
        nt, np_ = len(turns), len(products)
        with nc.Block() as block:

            @block.sync
            def _(sp):
                sp.wait_ge(cleared, 1)
                with nc.allow_non_contiguous_dma(reason="vectors of weights to columns"):
                    for to, of in loads:
                        sp.dma_start(to, of).then_inc(loaded, 16)
                sp.wait_ge(split, 5)
                for i, (upper, lower) in enumerate(((0, 0), (1, 1), (0, 2))):
                    sp.dma_start(core.w_stack[0:D, i, :], parts[:, upper, :]).then_inc(stacked, 16)
                    sp.dma_start(core.w_stack[D:2 * D, i, :], parts[:, lower, :]).then_inc(stacked, 16)
                sp.wait_ge(stacked, 16 * 6)

            @block.vector
            def _(v):
                v.memset(att_raw[:, :, :], 0.0).then_inc(cleared, 1)
                v.wait_ge(loaded, 16 * len(loads))
                v.tensor_scalar(core.att1[:, :, :], att_raw[:, :, :], 1.0 - SLOPE, None, ALU.mult)
                v.tensor_scalar(core.att2[:, :], att2_raw[:, :], 1.0 - SLOPE, None, ALU.mult)
                for i, (w, k, m) in enumerate(turns):
                    v.wait_ge(pe_done, i + 1)
                    v.tensor_copy(turned_w[0:m, i, 0:k], tmp[i % 2][0:m, 0:k]).then_inc(taken, 1)
                for i, (_, m, n, to, factor) in enumerate(products):
                    v.wait_ge(pe_done, nt + i + 1)
                    v.tensor_scalar(to, tmp[(nt + i) % 2][0:m, 0:n], factor, None, ALU.mult).then_inc(taken, 1)
                v.wait_ge(taken, nt + np_)
                v.tensor_copy(parts[:, 0, :], core.w_basis[:, :]).then_inc(split, 1)
                v.wait_ge(split, 1)
                v.tensor_tensor(rest[:, :], core.w_basis[:, :], parts[:, 0, :], ALU.subtract).then_inc(split, 1)
                v.wait_ge(split, 2)
                v.tensor_copy(parts[:, 1, :], rest[:, :]).then_inc(split, 1)
                v.wait_ge(split, 3)
                v.tensor_tensor(rest[:, :], rest[:, :], parts[:, 1, :], ALU.subtract).then_inc(split, 1)
                v.wait_ge(split, 4)
                v.tensor_copy(parts[:, 2, :], rest[:, :]).then_inc(split, 1)

            @block.tensor
            def _(pe):
                pe.wait_ge(loaded, 16 * len(loads))
                for i, (w, k, m) in enumerate(turns):
                    if i >= 2:
                        pe.wait_ge(taken, i - 1)
                    pe.transpose(tmp[i % 2][0:m, 0:k], w, core.ident[0:k, 0:k]).then_inc(pe_done, 1)
                pe.wait_ge(taken, nt)
                for i, (pairs, m, n, _, _) in enumerate(products):
                    if i >= 2:
                        pe.wait_ge(taken, nt + i - 1)
                    for j, (left, right) in enumerate(pairs):
                        mm = nc.tensor.matmul(tmp[(nt + i) % 2][0:m, 0:n], left, right, start=(j == 0),
                                              stop=(j == len(pairs) - 1))
                    mm.then_inc(pe_done, 1)


def normalise(core, tag, h_t):
    nc = core.nc
    with Stage(nc, tag) as st:
        mean, var, std, rstd = (st.sb(n, [ET, NT]) for n in ("mean", "var", "std", "rstd"))
        sq = st.sb("sq", [ET, NT, D])
        tp = [st.bank(f"tp{i}")[0:D, :].rearrange("c (t p) -> c t p", p=P) for i in range(2)]
        step, root, normed, turned, taken = (st.sem(n) for n in ("step", "root", "normed", "turned", "taken"))
        groups = [range(g, min(g + 4, NT)) for g in range(0, NT, 4)] if h_t is not None else []
        with nc.Block() as block:

            @block.vector
            def _(v):
                def wide(c):
                    return c[:, :].unsqueeze(2).to_broadcast([ET, NT, D])

                v.tensor_reduce(mean[:, :], core.x[:, :, :], AX_X, ALU.add).then_inc(step, 1)
                v.wait_ge(step, 1)
                v.tensor_scalar(mean[:, :], mean[:, :], 1.0 / D, None, ALU.mult).then_inc(step, 1)
                v.wait_ge(step, 2)
                v.tensor_tensor(core.h[:, :, :], core.x[:, :, :], wide(mean), ALU.subtract).then_inc(step, 1)
                v.wait_ge(step, 3)
                v.tensor_tensor(sq[:, :, :], core.h[:, :, :], core.h[:, :, :], ALU.mult).then_inc(step, 1)
                v.wait_ge(step, 4)
                v.tensor_reduce(var[:, :], sq[:, :, :], AX_X, ALU.add).then_inc(step, 1)
                v.wait_ge(step, 5)
                v.tensor_scalar(var[:, :], var[:, :], 1.0 / D, EPS, ALU.mult, ALU.add).then_inc(step, 1)
                v.wait_ge(root, 1)
                v.reciprocal(rstd[:, :], std[:, :]).then_inc(step, 1)
                v.wait_ge(step, 7)
                v.tensor_tensor(core.h[:, :, :], core.h[:, :, :], wide(rstd), ALU.mult).then_inc(step, 1)
                v.wait_ge(step, 8)
                v.tensor_scalar(core.h[:, :, :], core.h[:, :, :], 0.0, None, ALU.max).then_inc(normed, 1)

            @block.scalar
            def _(act):
                act.wait_ge(step, 6)
                act.activation(std[:, :], var[:, :], ACT.Sqrt).then_inc(root, 1)
                for g, tiles in enumerate(groups):
                    act.wait_ge(turned, g + 1)
                    n = len(tiles) * ET
                    act.copy(h_t[:, tiles[0] * ET:tiles[0] * ET + n].rearrange("c (t p) -> c t p", p=ET),
                             tp[g % 2][:, 0:len(tiles), 0:ET]).then_inc(taken, 1)

            @block.tensor
            def _(pe):
                for g, tiles in enumerate(groups):
                    if g == 0:
                        pe.wait_ge(normed, 1)
                    if g >= 2:
                        pe.wait_ge(taken, g - 1)
                    for i, t in enumerate(tiles):
                        mm = pe.transpose(tp[g % 2][:, i, 0:ET], core.h[:, t, :], core.ident[0:ET, 0:ET])
                    mm.then_inc(turned, 1)


def node_tables(core, tag, lhs, products, bias, width, rows, split, fill, stores):
    nc = core.nc
    with Stage(nc, tag) as st:
        row = st.sb("row", [ET, NT, width]) if width else None
        sr, s0, s1 = split
        sw = max(2, s1 - s0)
        part = st.sb("part", [ET, PARTS, NT + PADT, sw], BF16)
        rest = st.sb("rest", [ET, 2, s1 - s0])
        res = [[st.bank(f"res{i}_{r}")[0:ET, :] for r in range(len(products))] for i in range(2)]
        made, rows_done, hi, mid, taken, rest_done, filled, stored = (
            st.sem(n) for n in ("made", "rows_done", "hi", "mid", "taken", "rest_done", "filled", "stored"))
        out = stores(row, part)
        with nc.Block() as block:

            @block.tensor
            def _(pe):
                for t in range(NT):
                    if t >= 2:
                        pe.wait_ge(taken, t - 1)
                        pe.wait_ge(hi, t - 1)
                    for r, weights in enumerate(products):
                        n = weights[0].shape[-1]
                        for c, w in enumerate(weights):
                            mm = pe.matmul(res[t % 2][r][:, 0:n], lhs(c, t), w, start=(c == 0),
                                           stop=(c == len(weights) - 1 and (bias is None or r > 0)))
                        if bias is not None and r == 0:
                            mm = pe.matmul(res[t % 2][r][:, 0:n], core.ones[0:1, 0:ET], bias, start=False, stop=True)
                    mm.then_inc(made, 1)

            @block.scalar
            def _(act):
                for t in range(NT):
                    act.wait_ge(made, t + 1)
                    for (r, c0, c1, at) in rows:
                        act.copy(row[:, t, at:at + c1 - c0], res[t % 2][r][:, c0:c1])
                    act.copy(part[:, 0, t, 0:s1 - s0], res[t % 2][sr][:, s0:s1]).then_inc(hi, 1)
                    act.wait_ge(rest_done, t + 1)
                    act.copy(part[:, 1, t, 0:s1 - s0], rest[:, t % 2, :]).then_inc(mid, 1)

            @block.vector
            def _(v):
                for t in range(NT):
                    v.wait_ge(hi, t + 1)
                    v.tensor_tensor(rest[:, t % 2, :], res[t % 2][sr][:, s0:s1], part[:, 0, t, 0:s1 - s0],
                                    ALU.subtract).then_inc(rest_done, 1)
                    v.wait_ge(mid, t + 1)
                    v.wait_ge(rest_done, t + 1)
                    v.tensor_tensor(part[:, 2, t, 0:s1 - s0], rest[:, t % 2, :], part[:, 1, t, 0:s1 - s0],
                                    ALU.subtract).then_inc(taken, 1)

            @block.gpsimd
            def _(pool):
                fill(pool, row)
                if sw > s1 - s0:
                    pool.memset(part[:, :, 0:NT, s1 - s0:sw], 0.0)
                pool.memset(part[:, :, NT:NT + PADT, :], 0.0).then_inc(filled, 1)


            @block.sync
            def _(sp):
                sp.wait_ge(taken, NT)
                sp.wait_ge(mid, NT)
                sp.wait_ge(filled, 1)
                for to, of in out:
                    sp.dma_start(to, of).then_inc(stored, 16)
                sp.wait_ge(stored, 16 * len(out))


def node_rows(table, cols):
    return table.rearrange("(t p) c -> p t c", p=ET)[:, :, cols[0]:cols[1]]


def window_stores(table, part):
    return [(table[:, q, :].rearrange("(t p) c -> p t c", p=ET), part[:, q, :, :]) for q in range(PARTS)]


def load_window(eng, windows, table, at, win):
    if win == NARROW:
        return eng.dma_start(windows[:, 0, :], table.rearrange("n q c -> (n q) c")[bass.ds(at * PARTS, PARTS * win), :])
    return eng.dma_start(windows, table[bass.ds(at, win), :, :])


class Pass:

    def __init__(self, tag, rows, width, heads=0, relu=None, window=None, a_at=0, chunks=((0, D),), table_dt=F32):
        self.tag = tag
        self.rows = rows
        self.width = width
        self.heads = heads
        self.relu = relu
        self.window = window
        self.a_at = a_at
        self.chunks = chunks


def wait(eng, sem, value, met=None):
    if not isinstance(value, int) or value > 0:
        if met is not None and not isinstance(value, int):
            value = eng.compute_val(value)
            eng.wait_ge(met, 16)
        eng.wait_ge(sem, value)


def ring_blocks(eng, body):
    rings = BLOCKS // RING
    for s in range(RING):
        body(s, s, 0)
    with eng.Fori(1, rings - 1) as q:
        for s in range(RING):
            body(q * RING + s, s, q)
    for s in range(RING):
        body((rings - 1) * RING + s, s, rings - 1)


def edge_pass(core, ps_, win, acc, den):
    nc, a = core.nc, core.a
    H, att = ps_.heads, ps_.heads > 0
    many = H == HEADS
    gat = ps_.relu is not None
    CH = WIDE // P if many else 1
    CW = P if many else D
    stack = win == NARROW
    K = PARTS * win if stack else win
    NPART = 1 if stack else PARTS
    XR = RING if stack else 1
    FW = ps_.window.shape[2] if att else 0
    WA = CW * CH if gat else 0
    AW = acc.shape[0]
    with Stage(nc, f"{ps_.tag}{win}") as st:
        idx = st.sb("idx", [P, RING, BT], I32)
        src_rows = st.sb("src_rows", [P, RING, BT, ps_.width])
        onehot = st.sb("onehot", [ET, BT, win])
        weighted = st.sb("weighted", [ET, BT, max(H, 1), win])
        idx_in = [st.sem(f"idx_in{s}") for s in range(RING)]
        gathered, sofar = core.gathered, core.sofar
        core.sofar += BLOCKS // RING * BT * 16
        onehot_done, weighted_done, agg_done, upd_done = (
            st.sem(n) for n in ("onehot_done", "weighted_done", "agg_done", "upd_done"))
        agg = [st.bank(f"agg{i}") for i in range(2)]
        if att:
            rel_b = st.sb("rel_b", [K, XR, BE], BF16)
            reset = st.sb("reset", [H, XR, BE + 1], BF16)
            windows = st.sb("windows", [K, XR, BT, NPART, FW], BF16)
            spread = st.sb("spread", [K, RING, BE], BF16)
            logit = st.sb("logit", [H, RING, BE])
            fore = st.sb("fore", [H, BE])
            top = st.sb("top", [H, BE])
            carry = st.sb("carry", [H, RING])
            fade_in = st.sb("fade_in", [H, RING])
            fade = st.sb("fade", [H, RING])
            prob = st.sb("prob", [ET, RING, BT, H])
            fade_w = st.sb("fade_w", [P, RING, 4])
            rows_in = [st.sem(f"rows_in{s}") for s in range(RING)]
            win_in = [st.sem(f"win_in{s}") for s in range(XR)]
            (spread_done, e_done, copied, fore_done, top_done, carried, shifted, fade_max, fade_set, faded,
             fade_wide, fade_taken, back_done, prob_done, scaled, base_done) = (
                st.sem(n) for n in ("spread_done", "e_done", "copied", "fore_done", "top_done", "carried", "shifted",
                                    "fade_max", "fade_set", "faded", "fade_wide", "fade_taken", "back_done",
                                    "prob_done", "scaled", "base_done"))
            e_ps = [st.bank(f"e{i}")[0:H, :] for i in range(2)]
            back_ps = st.bank("back")[0:ET, 0:BT * H]
            fade_bank = st.bank("fade")
            fade_ps = fade_bank[:, 0:4]
            den_own = 4 * win + win > 512
            den_ps = [fade_bank[0:H, FULL:FULL + win] if den_own else agg[i][0:H, 4 * win:5 * win] for i in range(2)]
            base = st.sb("base", [ET, RING, BT, H])
        if gat:
            m_ps = [st.bank(f"m{i}")[0:CW, 0:CH * P].rearrange("c (h e) -> c h e", h=CH) for i in range(2)]
            pos = st.sb("pos", [CW, 2, CH, ET])
            m_done, pos_done, counted = st.sem("m_done"), st.sem("pos_done"), st.sem("counted")

        e_groups = [(g, min(g + 4, BT)) for g in range(0, BT, 4)]


        with nc.Block() as block:

            @block.sync
            def _(sp):
                def body(k, s, q):
                    wait(sp, gathered[s], sofar + q * (16 * BT))
                    sp.dma_start(idx[:, s, :], a["src_t"][:, bass.ds(k * BT, BT)]).then_inc(idx_in[s], 16)
                    if not att:
                        return
                    wait(sp, spread_done, k - (XR - 1))
                    sp.dma_start(rel_b[:, s % XR, :], core.rel_rows[bass.ds(k, 1), :].to_broadcast([K, BE])
                                 ).then_inc(rows_in[s], 16)
                    wait(sp, top_done, k - (XR - 1))
                    sp.dma_start(reset[:, s % XR, :], core.reset_rows[bass.ds(k, 1), :].to_broadcast([H, BE + 1])
                                 ).then_inc(rows_in[s], 16)
                    wait(sp, e_done, (k - (XR - 1)) * BT, met=idx_in[s])
                    for j in range(BT):
                        at = sp.value_load(core.first[0:1, bass.ds(k * BT + j, 1)], min_val=0, max_val=N - 1)
                        load_window(sp, windows[:, s % XR, j, :, :], ps_.window, at, win).then_inc(win_in[s % XR], 16)
                ring_blocks(sp, body)

            @block.gpsimd
            def _(pool):
                def body(k, s, q):
                    wait(pool, idx_in[s], q * 16 + 16, met=idx_in[s])
                    for j in range(BT):
                        wait(pool, agg_done, (k - RING) * BT + j + 1, met=idx_in[s])
                        pool.indirect_dma_start(src_rows[:, s, j, :], None, ps_.rows,
                                                bass.IndirectOffsetOnAxis(ap=idx[:, s, j:j + 1], axis=0)
                                                ).then_inc(gathered[s], 16)
                ring_blocks(pool, body)

            @block.tensor
            def _(pe):
                def logits(k, s, j):
                    g, i = j // 4, j % 4
                    if i == 0:
                        wait(pe, copied, k * len(e_groups) + (1 if g == 2 else 0))
                    if gat:
                        pe.wait_ge(pos_done, k * BT + j + 1)
                        extra = src_rows[0:ET, s, j, ps_.a_at:ps_.a_at + H]
                    else:
                        extra = base[:, s, j, :]
                    to = e_ps[g % 2][:, i * ET:(i + 1) * ET]
                    pe.matmul(to, extra, core.ident[0:ET, 0:ET], start=True, stop=False, is_transpose=True)
                    for w in range(NPART):
                        mm = pe.matmul(to, windows[:, s % XR, j, w, WA:WA + H],
                                       spread[:, s, j * ET:(j + 1) * ET], start=False,
                                       stop=(not gat and w == NPART - 1))
                    if gat:
                        for c in range(CH):
                            mm = pe.matmul(to, ps_.relu[:, c, :] if many else ps_.relu[:, :], pos[:, j % 2, c, :],
                                           start=False, stop=(c == CH - 1))
                    mm.then_inc(e_done, 1)

                def stage1(k, s, q):
                    wait(pe, gathered[s], sofar + q * (16 * BT) + 16 * BT, met=idx_in[s])
                    n_win = BT * 16
                    if stack:
                        pe.wait_ge(win_in[s], q * n_win + n_win)
                    else:
                        pe.wait_ge(win_in[0], k * n_win + n_win)
                    pe.wait_ge(spread_done, k + 1)
                    if not gat:
                        pe.wait_ge(base_done, k + 1)
                    for j in range(BT):
                        if gat:
                            wait(pe, pos_done, k * BT + (j - 1 if j else 0), met=None if many else idx_in[s])
                            for c in range(CH):
                                to = m_ps[j % 2][:, c, 0:ET]
                                pe.matmul(to, src_rows[0:ET, s, j, ps_.chunks[c][0]:ps_.chunks[c][0] + CW],
                                          core.ident[0:ET, 0:ET], start=True, stop=False, is_transpose=True)
                                for w in range(NPART):
                                    mm = pe.matmul(to, windows[:, s % XR, j, w, c * CW:(c + 1) * CW],
                                                   spread[:, s, j * ET:(j + 1) * ET], start=False,
                                                   stop=(w == NPART - 1))
                            mm.then_inc(m_done, 1)
                            if j:
                                logits(k, s, j - 1)
                        else:
                            logits(k, s, j)
                    if gat:
                        logits(k, s, BT - 1)

                def aggregate(k, s):
                    pe.wait_ge(weighted_done, k + 1)
                    for j in range(BT):
                        wait(pe, upd_done, k * BT + (j - 1 if j else 0))
                        slot = j % 2
                        if many:
                            for c in range(CH):
                                c0 = ps_.chunks[c][0]
                                pe.matmul(agg[slot][:, c * 2 * win:(c + 1) * 2 * win],
                                          src_rows[0:ET, s, j, c0:c0 + CW],
                                          weighted[:, j, 2 * c:2 * c + 2, :], start=True, stop=True)
                            if den_own:
                                wait(pe, upd_done, k * BT + j)
                                pe.wait_ge(fade_taken, k + 1)
                            mm = pe.matmul(den_ps[slot], prob[:, s, j, :], onehot[:, j, :], start=True, stop=True)
                        else:
                            mm = pe.matmul(agg[slot][0:AW, 0:win], src_rows[0:ET, s, j, 0:AW],
                                           weighted[:, j, 0, :], start=True, stop=True)
                        mm.then_inc(agg_done, 1)

                def turn_back(k, s):
                    wait(pe, shifted, k + 1, met=idx_in[s])
                    wait(pe, prob_done, k)
                    for j in range(BT):
                        mm = pe.transpose(back_ps[:, j * H:(j + 1) * H], logit[:, s, j * ET:(j + 1) * ET],
                                          core.ident[0:H, 0:H])
                    mm.then_inc(back_done, 1)
                    pe.wait_ge(faded, k + 1)
                    if many and den_own:
                        wait(pe, upd_done, k * BT)
                    wait(pe, fade_taken, k)
                    if many:
                        for c in range(CH):
                            mm = pe.matmul(fade_ps[:, c:c + 1], core.head_of[:, c, :], fade[:, s:s + 1],
                                           start=True, stop=True)
                    else:
                        mm = pe.matmul(fade_ps[:, 0:1], core.ones[0:1, :], fade[:, s:s + 1], start=True, stop=True)
                    mm.then_inc(fade_wide, 1)

                def body(k, s, q):
                    if att:
                        stage1(k, s, q)
                        if not isinstance(k, int) or k > 0:
                            aggregate(k - 1, (s - 1) % RING)
                        turn_back(k, s)
                    else:
                        pe.wait_ge(gathered[s], sofar + q * (16 * BT) + 16 * BT)
                        aggregate(k, s)
                ring_blocks(pe, body)
                if att:
                    aggregate(BLOCKS - 1, RING - 1)

            @block.scalar
            def _(act):
                def body(k, s, q):
                    def copy(g):
                        lo, hi = e_groups[g]
                        act.wait_ge(e_done, k * BT + hi)
                        if g == 0:
                            wait(act, back_done, k - (RING - 1))
                        act.copy(logit[:, s, lo * ET:hi * ET], e_ps[g % 2][:, 0:(hi - lo) * ET]).then_inc(copied, 1)

                    nxt = 0
                    if gat:
                        for j in range(BT):
                            act.wait_ge(m_done, k * BT + j + 1)
                            wait(act, e_done, k * BT + (j - 1 if j else 0))
                            act.activation(pos[:, j % 2, :, :], m_ps[j % 2][:, :, 0:ET], ACT.Relu).then_inc(pos_done, 1)
                            if nxt < len(e_groups) and j >= e_groups[nxt][1] + 1:
                                copy(nxt)
                                nxt += 1
                    for g in range(nxt, len(e_groups)):
                        copy(g)
                    act.wait_ge(fade_set, k + 1)
                    wait(act, fade_wide, k - (RING - 1))
                    act.activation(fade[:, s:s + 1], fade_in[:, s:s + 1], ACT.Exp).then_inc(faded, 1)
                    act.wait_ge(back_done, k + 1)
                    wait(act, agg_done, (k - (RING - 1)) * BT)
                    act.activation(prob[:, s, :, :].rearrange("p t h -> p (t h)"), back_ps, ACT.Exp
                                   ).then_inc(prob_done, 1)
                if att:
                    ring_blocks(act, body)

            @block.vector
            def _(v):
                def update(k, j):
                    at = v.value_load(core.first[0:1, bass.ds(k * BT + j, 1)], min_val=0, max_val=N - 1)
                    v.wait_ge(agg_done, k * BT + j + 1)
                    wait(v, upd_done, k * BT + j)
                    if many:
                        sums = agg[j % 2][:, 0:CH * 2 * win].rearrange("p (x j) -> p x j", j=win)
                        for half in range(2):
                            lo = half * D
                            to = acc[lo:lo + D, :, bass.ds(at, win)]
                            v.tensor_tensor(to, to, sums[lo:lo + D, half:half + 3:2, :], ALU.add)
                        to = den[:, bass.ds(at, win)]
                        v.tensor_tensor(to, to, den_ps[j % 2], ALU.add).then_inc(upd_done, 1)
                    else:
                        to = acc[:, bass.ds(at, win)]
                        v.tensor_tensor(to, to, agg[j % 2][0:AW, 0:win], ALU.add).then_inc(upd_done, 1)

                def make_onehot(k):
                    if many:
                        wait(v, agg_done, k * BT)
                    wait(v, weighted_done, k)
                    v.tensor_tensor(onehot[:, :, :],
                                    core.iota_row[0:ET, 0:win].unsqueeze(1).to_broadcast([ET, BT, win]),
                                    core.rel[:, bass.ds(k * BT, BT)].unsqueeze(2).to_broadcast([ET, BT, win]),
                                    ALU.is_equal).then_inc(onehot_done, 1)

                def weigh(k, weights):
                    wait(v, agg_done, k * BT)
                    v.wait_ge(onehot_done, k + 1)
                    h = max(H, 1)
                    v.tensor_tensor(weighted[:, :, :, :],
                                    onehot[:, :, :].unsqueeze(2).to_broadcast([ET, BT, h, win]),
                                    weights.unsqueeze(3).to_broadcast([ET, BT, h, win]),
                                    ALU.mult).then_inc(weighted_done, 1)

                def make_spread(k, s, q):
                    v.wait_ge(rows_in[s], q * 32 + 32)
                    wait(v, e_done, (k - (RING - 1)) * BT)
                    v.tensor_scalar(spread[:, s, :], rel_b[:, s % XR, :], core.iota_col[0:K, 1 if stack else 0:][:, 0:1],
                                    None, ALU.is_equal).then_inc(spread_done, 1)

                def make_base(k, s, q):
                    v.wait_ge(gathered[s], sofar + q * (16 * BT) + 16 * BT)
                    v.tensor_tensor(base[:, s, :, 0], src_rows[0:ET, s, :, ps_.a_at],
                                    core.relw[:, bass.ds(k * BT, BT)], ALU.add).then_inc(base_done, 1)

                def ahead(k, s, q):
                    make_spread(k, s, q)
                    if not gat:
                        make_base(k, s, q)

                def fade_sums(k, s):
                    v.wait_ge(fade_wide, k + 1)
                    v.tensor_copy(fade_w[:, s, 0:CH], fade_ps[:, 0:CH]).then_inc(fade_taken, 1)
                    at = v.value_load(core.first[0:1, bass.ds(k * BT, 1)], min_val=0, max_val=N - 1)
                    v.wait_ge(fade_taken, k + 1)
                    wait(v, upd_done, k * BT)
                    if many:
                        for c in range(CH):
                            to = acc[:, c, bass.ds(at, 1)]
                            v.tensor_tensor(to, to, fade_w[:, s, c:c + 1], ALU.mult)
                        to = den[:, bass.ds(at, 1)]
                        v.tensor_tensor(to, to, fade[:, s:s + 1], ALU.mult).then_inc(scaled, 1)
                    else:
                        to = acc[:, bass.ds(at, 1)]
                        v.tensor_tensor(to, to, fade_w[0:AW, s, 0:1], ALU.mult).then_inc(scaled, 1)
                    v.wait_ge(scaled, k + 1)

                def body(k, s, q):
                    more = not isinstance(k, int) or k > 0
                    if not att:
                        make_onehot(k)
                        weigh(k, core.ew[:, bass.ds(k * BT, BT)].unsqueeze(2))
                        for j in range(BT):
                            update(k, j)
                        return
                    if not more:
                        ahead(k, s, q)
                    if more:
                        fade_sums(k - 1, (s - 1) % RING)
                    v.wait_ge(copied, (k + 1) * len(e_groups))
                    v.wait_ge(rows_in[s], q * 32 + 32)
                    if more:
                        v.wait_ge(carried, k)
                    v.tensor_tensor_scan(fore[:, :], reset[:, s % XR, 0:BE], logit[:, s, :],
                                         carry[:, (s - 1) % RING:(s - 1) % RING + 1] if more else -BIG,
                                         ALU.add, ALU.max).then_inc(fore_done, 1)
                    if more:
                        for j in range(0, 4):
                            update(k - 1, j)
                    v.wait_ge(fore_done, k + 1)
                    v.tensor_copy(carry[:, s:s + 1], fore[:, BE - 1:BE]).then_inc(carried, 1)
                    v.tensor_tensor_scan(top[:, ::-1], reset[:, s % XR, BE:0:-1], fore[:, ::-1], -BIG,
                                         ALU.add, ALU.max).then_inc(top_done, 1)
                    if more:
                        for j in range(4, 8):
                            update(k - 1, j)
                    v.wait_ge(top_done, k + 1)
                    v.tensor_tensor(logit[:, s, :], logit[:, s, :], top[:, :], ALU.subtract).then_inc(shifted, 1)
                    if more:
                        v.tensor_tensor(fade_in[:, s:s + 1], carry[:, (s - 1) % RING:(s - 1) % RING + 1], top[:, 0:1],
                                        ALU.subtract).then_inc(fade_max, 1)
                    else:
                        v.memset(fade_in[:, s:s + 1], 0.0).then_inc(fade_max, 1)
                    v.wait_ge(fade_max, k + 1)
                    v.tensor_scalar(fade_in[:, s:s + 1], fade_in[:, s:s + 1], 0.0, None, ALU.min).then_inc(fade_set, 1)
                    if more:
                        for j in range(8, BT):
                            update(k - 1, j)
                    make_onehot(k)
                    if not isinstance(k, int) or k + 1 < BLOCKS:
                        ahead(k + 1, (s + 1) % RING, q + (s + 1) // RING)
                    v.wait_ge(prob_done, k + 1)
                    if gat:
                        v.tensor_tensor(prob[:, s, :, :], prob[:, s, :, :],
                                        core.times[:, bass.ds(k * BT, BT)].unsqueeze(2).to_broadcast([ET, BT, H]),
                                        ALU.mult).then_inc(counted, 1)
                        v.wait_ge(counted, k + 1)
                    weigh(k, prob[:, s, :, :])
                ring_blocks(v, body)
                if att:
                    fade_sums(BLOCKS - 1, RING - 1)
                    for j in range(BT):
                        update(BLOCKS - 1, j)


def clear_sums(core, tag, tensors):
    nc = core.nc
    with Stage(nc, tag) as st:
        done = st.sem("done")
        with nc.Block() as block:

            @block.gpsimd
            def _(pool):
                for t in tensors:
                    pool.memset(t, 0.0).then_inc(done, 1)
                pool.wait_ge(done, len(tensors))


def finish_gat1(core, win, acc, den):
    nc = core.nc
    STEP = 4 * ET
    pieces = [(c, n, min(n + STEP, N)) for c in range(2) for n in range(0, N, STEP)]
    with Stage(nc, f"fin1_{win}") as st:
        wide = [st.bank(f"wide{i}") for i in range(2)]
        inv, spread, mult, out = (st.sem(n) for n in ("inv", "spread", "mult", "out"))
        with nc.Block() as block:

            @block.tensor
            def _(pe):
                pe.wait_ge(inv, 2)
                for i, (c, lo, hi) in enumerate(pieces):
                    if i >= 2:
                        pe.wait_ge(mult, i - 1)
                    pe.matmul(wide[i % 2][:, 0:hi - lo], core.head_of[:, c, :], den[:, lo:hi], start=True,
                              stop=True).then_inc(spread, 1)

            @block.vector
            def _(v):
                v.tensor_scalar(den[:, 0:N], den[:, 0:N], TINY, None, ALU.max).then_inc(inv, 1)
                v.wait_ge(inv, 1)
                v.reciprocal(den[:, 0:N], den[:, 0:N]).then_inc(inv, 1)
                for i, (c, lo, hi) in enumerate(pieces):
                    v.wait_ge(spread, i + 1)
                    v.tensor_tensor(acc[:, c, lo:hi], acc[:, c, lo:hi], wide[i % 2][:, 0:hi - lo],
                                    ALU.mult).then_inc(mult, 1)

            @block.scalar
            def _(act):
                for i, (c, lo, hi) in enumerate(pieces):
                    act.wait_ge(mult, i + 1)
                    act.activation(acc[:, c, lo:hi], acc[:, c, lo:hi], ACT.Gelu, bias=core.b1[:, c:c + 1]).then_inc(out, 1)


def finish_narrow(core, tag, acc, kind, g, store=None):
    nc = core.nc
    AW = acc.shape[0]
    groups = [range(n, min(n + 7, NT)) for n in range(0, NT, 7)]
    with Stage(nc, tag) as st:
        back = [st.bank(f"back{i}")[0:ET, :] for i in range(2)]
        mean = st.sb("mean", [ET, NT, D])
        inv = st.sb("inv", [ET, NT])
        turned, step, taken, stored = (st.sem(n) for n in ("turned", "step", "taken", "stored"))
        with nc.Block() as block:

            @block.tensor
            def _(pe):
                for n, tiles in enumerate(groups):
                    if n >= 2:
                        pe.wait_ge(taken, n - 1)
                    for i, t in enumerate(tiles):
                        mm = pe.transpose(back[n % 2][:, i * AW:(i + 1) * AW], acc[:, t * ET:(t + 1) * ET],
                                          core.ident[0:AW, 0:AW])
                    mm.then_inc(turned, 1)

            @block.vector
            def _(v):
                count = [0]

                def then(ins):
                    count[0] += 1
                    ins.then_inc(step, 1)
                    v.wait_ge(step, count[0])

                for n, tiles in enumerate(groups):
                    t0, t1 = tiles[0], tiles[-1] + 1
                    w = t1 - t0
                    b3 = back[n % 2][:, 0:w * AW].rearrange("p (t c) -> p t c", c=AW)
                    v.wait_ge(turned, n + 1)
                    if kind == "gcn":
                        v.tensor_copy(mean[:, t0:t1, :], b3[:, :, 0:D]).then_inc(taken, 1)
                    else:
                        cnt = b3[:, :, D]
                        if kind == "mean, edges":
                            then(v.tensor_scalar(core.has_edges[:, t0:t1], cnt, 0.0, None, ALU.is_gt))
                        then(v.tensor_scalar(inv[:, t0:t1], cnt, TINY, None, ALU.max))
                        then(v.reciprocal(inv[:, t0:t1], inv[:, t0:t1]))
                        v.tensor_tensor(mean[:, t0:t1, :], b3[:, :, 0:D],
                                        inv[:, t0:t1].unsqueeze(2).to_broadcast([ET, w, D]), ALU.mult).then_inc(taken, 1)
                v.wait_ge(taken, len(groups))
                if kind == "gcn":
                    last = g["last"]
                    old, new = g["old"], g["new"]
                    then(v.tensor_tensor(mean[:, :, :], mean[:, :, :], old, ALU.subtract))
                    then(v.tensor_tensor(mean[:, :, :], mean[:, :, :],
                                         core.has_edges[:, :].unsqueeze(2).to_broadcast([ET, NT, D]), ALU.mult))
                    then(v.tensor_scalar(mean[:, :, :], mean[:, :, :], 0.5, None, ALU.mult))
                    then(v.tensor_tensor(new, mean[:, :, :], old, ALU.add))
                    if last:
                        then(v.tensor_tensor(core.x[:, :, :], core.x[:, :, :], new, ALU.add))
                else:
                    if kind == "mean, bias":
                        then(v.tensor_tensor(mean[:, :, :], mean[:, :, :],
                                             core.b2[:, :].unsqueeze(1).to_broadcast([ET, NT, D]), ALU.add))
                    then(v.tensor_tensor(core.x[:, :, :], core.x[:, :, :], mean[:, :, :], ALU.add))

            if store is not None:
                @block.sync
                def _(sp):
                    sp.wait_ge(step, 4)
                    sp.dma_start(store[0], store[1]).then_inc(stored, 16)
                    sp.wait_ge(stored, 16)


def pair_tables(core, win, h_t):
    nc = core.nc
    STEP = 4 * ET
    pieces = [(n, min(n + STEP, N)) for n in range(0, N, STEP)]
    with ExitStack() as ctx:
        p1 = ctx.enter_context(nc.sbuf_tensor(f"pair_p1_{win}", [D, N], F32))
        v_t = ctx.enter_context(nc.sbuf_tensor(f"pair_v_{win}", [D, N], F32))
        with Stage(nc, f"pair_{win}") as st:
            ps = [st.bank(f"p{i}")[0:D, :] for i in range(2)]
            made, taken = st.sem("made"), st.sem("taken")
            with nc.Block() as block:

                @block.tensor
                def _(pe):
                    m = len(pieces)
                    for i, (w, src, (lo, hi)) in enumerate([(core.w_pp[:, :], h_t, p) for p in pieces]
                                                           + [(core.w_pair[:, 1, :], p1, p) for p in pieces]):
                        if i >= 2:
                            pe.wait_ge(taken, i - 1)
                        if i >= m:
                            pe.wait_ge(taken, i - m + 1)
                        pe.matmul(ps[i % 2][:, 0:hi - lo], w, src[:, lo:hi], start=True, stop=True).then_inc(made, 1)

                @block.scalar
                def _(act):
                    for i, (lo, hi) in enumerate(pieces):
                        act.wait_ge(made, i + 1)
                        act.activation(p1[:, lo:hi], ps[i % 2][:, 0:hi - lo], ACT.Tanh, bias=core.b_pp[:, 0:1]
                                       ).then_inc(taken, 1)
                    for i, (lo, hi) in enumerate(pieces):
                        act.wait_ge(made, len(pieces) + i + 1)
                        act.copy(v_t[:, lo:hi], ps[(len(pieces) + i) % 2][:, 0:hi - lo]).then_inc(taken, 1)
        node_tables(core, f"pair_u_{win}", lambda c, t: p1[:, t * ET:(t + 1) * ET], [[core.w_pair[:, 0, :]]],
                    core.b_pair[0:1, :], 0, [], (0, 0, D), lambda pool, row: None,
                    lambda row, part: [(node_rows(core.pair_rows, (i * D, (i + 1) * D)), part[:, q, 0:NT, :])
                                       for i, q in enumerate((0, 1, 2, 0))])
        node_tables(core, f"pair_w_{win}", lambda c, t: v_t[:, t * ET:(t + 1) * ET], [[core.w_basis[:, :]]],
                    None, 0, [], (0, 0, D * NBASIS), lambda pool, row: None,
                    lambda row, part: window_stores(core.pair_win, part))


def pair_pass(core, win):
    nc, a = core.nc, core.a
    stack = win == NARROW
    K = PARTS * win if stack else win
    NPART = 1 if stack else PARTS
    XR = RING if stack else 1
    DB = D * NBASIS
    with Stage(nc, f"pairs{win}") as st:
        idx = st.sb("idx", [P, RING, BT], I32)
        src_rows = st.sb("src_rows", [P, RING, BT, 4 * D], BF16)
        rel_b = st.sb("rel_b", [K, RING, BE], BF16)
        windows = st.sb("windows", [K, XR, BT, NPART, DB], BF16)
        spread = st.sb("spread", [K, RING, BE], BF16)
        basis = st.sb("basis", [ET, RING, BT, NBASIS])
        src_b = st.sb("src_b", [ET, RING, BE], I32)
        same = st.sb("same", [ET, RING, BT, ET])
        earlier = st.sb("earlier", [ET, BT, ET])
        before = st.sb("before", [ET, ET])
        seen = st.sb("seen", [ET, BT])
        src_f = st.sb("src_f", [ET, BT])
        away = st.sb("away", [ET, BT])
        to_rows = st.sb("to_rows", [P, RING, BT], I32)
        hid = st.sb("hid", [P, 2, 2, ET], BF16)
        prod = st.sb("prod", [ET, 2, D, NBASIS + 1])
        i1 = st.sb("i1", [ET, 2, D])
        i2 = st.sb("i2", [ET, 2, D])
        out = st.sb("out", [P, COPIES, D])
        idx_in = [st.sem(f"idx_in{s}") for s in range(RING)]
        rows_in = [st.sem(f"rows_in{s}") for s in range(RING)]
        gathered, sofar = core.gathered, core.sofar
        core.sofar += BLOCKS // RING * BT * 16
        win_in = [st.sem(f"win_in{s}") for s in range(XR)]
        scattered = core.scattered
        (spread_done, same_done, earlier_done, to_done, set_up, turned, hid_done, full_done, prod_done, i1_done,
         i2_done, sum_done, out_done, mask_in, step, bias_set) = (
            st.sem(n) for n in ("spread_done", "same_done", "earlier_done", "to_done", "set_up", "turned", "hid_done",
                                "full_done", "prod_done", "i1_done", "i2_done", "sum_done", "out_done", "mask_in",
                                "step", "bias_set"))
        turn_ps = [st.bank(f"turn{i}", BF16)[:, 0:2 * P].rearrange("p (h e) -> p h e", h=2) for i in range(2)]
        full = [st.bank(f"full{i}")[0:ET, :] for i in range(2)]
        sum_ps = [st.bank(f"sum{i}")[0:ET, 0:D] for i in range(2)]
        TANH_LAG, SUM_LAG, SCATTER_LAG = 1, 3, 5


        def used(k, j):
            return k * BT + (j - 1 if j else 0)

        def behind(k, s, j, lag):
            if j >= lag:
                return k, s, j - lag
            if isinstance(k, int) and k == 0:
                return None
            return k - 1, (s - 1) % RING, j - lag + BT

        with nc.Block() as block:

            @block.sync
            def _(sp):
                sp.dma_start(before[:, :], a["before"]).then_inc(mask_in, 16)
                sp.dma_start(to_rows[:, :, :].rearrange("p r t -> p (r t)"), a["spare_rows"]).then_inc(mask_in, 16)

                def body(k, s, q):
                    wait(sp, gathered[s], sofar + q * (16 * BT), met=idx_in[s])
                    wait(sp, to_done, k - (RING - 1), met=idx_in[s])
                    sp.dma_start(idx[:, s, :], a["src_t"][:, bass.ds(k * BT, BT)]).then_inc(idx_in[s], 16)
                    wait(sp, spread_done, k - (RING - 1))
                    sp.dma_start(rel_b[:, s, :], core.rel_rows[bass.ds(k, 1), :].to_broadcast([K, BE])
                                 ).then_inc(rows_in[s], 16)
                    wait(sp, same_done, k - (RING - 1), met=idx_in[s])
                    sp.dma_start(src_b[:, s, :], a["src"].rearrange("(k e) -> k e", k=BLOCKS)[bass.ds(k, 1), :]
                                 .to_broadcast([ET, BE])).then_inc(rows_in[s], 16)
                    wait(sp, prod_done, (k - (RING - 1)) * BT)
                    sp.dma_start(basis[:, s, :, :].rearrange("p t b -> p (t b)"),
                                 a["basis_t"][:, bass.ds(k * (BT * NBASIS), BT * NBASIS)]).then_inc(rows_in[s], 16)
                    wait(sp, full_done, (k - (XR - 1)) * BT, met=idx_in[s])
                    for j in range(BT):
                        at = sp.value_load(core.first[0:1, bass.ds(k * BT + j, 1)], min_val=0, max_val=N - 1)
                        load_window(sp, windows[:, s % XR, j, :, :], core.pair_win, at, win).then_inc(win_in[s % XR], 16)
                ring_blocks(sp, body)

            @block.gpsimd
            def _(pool):
                pool.memset(out[:, :, :], 0.0).then_inc(set_up, 1)
                pool.wait_ge(mask_in, 32)

                def gather(k, s, q, j):
                    if j == 0:
                        wait(pool, idx_in[s], q * 16 + 16, met=idx_in[s])
                    wait(pool, turned, (k - RING) * BT + j + 1, met=idx_in[s])
                    pool.indirect_dma_start(src_rows[:, s, j, :], None, core.pair_rows,
                                            bass.IndirectOffsetOnAxis(ap=idx[:, s, j:j + 1], axis=0)
                                            ).then_inc(gathered[s], 16)

                def scatter(k, s, q, j):
                    c, n = (s * BT + j) % COPIES, q * (RING * BT // COPIES) + (s * BT + j) // COPIES
                    if j == 0:
                        wait(pool, to_done, k + 1, met=idx_in[s])
                    wait(pool, out_done, k * BT + j + 1, met=idx_in[s])
                    wait(pool, scattered[c], n * 16, met=idx_in[s])
                    pool.indirect_dma_start(core.sums[c], bass.IndirectOffsetOnAxis(ap=to_rows[:, s, j:j + 1], axis=0),
                                            out[:, c, :], None, bounds_check=NP - 1, oob_is_err=True,
                                            compute_op=ALU.add).then_inc(scattered[c], 16)

                for j in range(BT):
                    gather(0, 0, 0, j)

                def body(k, s, q):
                    for j in range(BT):
                        if not isinstance(k, int) or k + 1 < BLOCKS:
                            gather(k + 1, (s + 1) % RING, q + (s + 1) // RING, j)
                        at = behind(k, s, j, SCATTER_LAG)
                        if at:
                            scatter(at[0], at[1], q - (at[1] > s), at[2])
                ring_blocks(pool, body)
                for j in range(BT - SCATTER_LAG, BT):
                    scatter(BLOCKS - 1, RING - 1, BLOCKS // RING - 1, j)
                for c in range(COPIES):
                    pool.wait_ge(scattered[c], 16 * (TILES // COPIES))

            @block.tensor
            def _(pe):
                def turn(k, s, q, j):
                    if j == 0:
                        pe.wait_ge(gathered[s], sofar + q * (16 * BT) + 16 * BT)
                    wait(pe, hid_done, used(k, j))
                    for h in range(2):
                        mm = pe.transpose(turn_ps[j % 2][:, h, 0:ET], src_rows[0:ET, s, j, h * P:(h + 1) * P],
                                          core.identb[0:ET, 0:ET])
                    mm.then_inc(turned, 1)

                def expand(k, s, q, j):
                    if j == 0:
                        pe.wait_ge(spread_done, k + 1)
                        n_win = BT * 16
                        if stack:
                            pe.wait_ge(win_in[s], q * n_win + n_win)
                        else:
                            pe.wait_ge(win_in[0], k * n_win + n_win)
                    pe.wait_ge(hid_done, k * BT + j + 1)
                    wait(pe, prod_done, used(k, j))
                    to = full[j % 2]
                    for i, h in enumerate((0, 0, 1)):
                        pe.matmul(to, hid[:, j % 2, h, :], core.w_stack[:, i, :], start=(i == 0), stop=False)
                    for w in range(NPART):
                        mm = pe.matmul(to, spread[:, s, j * ET:(j + 1) * ET], windows[:, s % XR, j, w, :],
                                       start=False, stop=(w == NPART - 1))
                    mm.then_inc(full_done, 1)

                def sum_same(k, s, j):
                    if j == 0:
                        pe.wait_ge(same_done, k + 1)
                    pe.wait_ge(i2_done, k * BT + j + 1)
                    wait(pe, out_done, used(k, j))
                    pe.matmul(sum_ps[j % 2], same[:, s, j, :], i2[:, j % 2, :], start=True, stop=True
                              ).then_inc(sum_done, 1)

                def body(k, s, q):
                    for j in range(BT):
                        turn(k, s, q, j)
                        at = behind(k, s, j, TANH_LAG)
                        if at:
                            expand(at[0], at[1], q - (at[1] > s), at[2])
                        at = behind(k, s, j, SUM_LAG)
                        if at:
                            sum_same(*at)
                ring_blocks(pe, body)
                expand(BLOCKS - 1, RING - 1, BLOCKS // RING - 1, BT - 1)
                for j in range(BT - SUM_LAG, BT):
                    sum_same(BLOCKS - 1, RING - 1, j)

            @block.scalar
            def _(act):
                def take(k, s, j):
                    act.wait_ge(turned, k * BT + j + 1)
                    wait(act, full_done, used(k, j))
                    act.copy(hid[:, j % 2, :, :], turn_ps[j % 2][:, :, 0:ET]).then_inc(hid_done, 1)

                def tanh(k, s, j):
                    act.wait_ge(i1_done, k * BT + j + 1)
                    wait(act, sum_done, used(k, j))
                    act.activation(i2[:, j % 2, :], i1[:, j % 2, :], ACT.Tanh).then_inc(i2_done, 1)

                def put_out(k, s, q, j):
                    c, n = (s * BT + j) % COPIES, q * (RING * BT // COPIES) + (s * BT + j) // COPIES
                    act.wait_ge(sum_done, k * BT + j + 1)
                    wait(act, scattered[c], n * 16)
                    act.copy(out[0:ET, c, :], sum_ps[j % 2]).then_inc(out_done, 1)

                def body(k, s, q):
                    if isinstance(k, int) and k == 0:
                        act.wait_ge(set_up, 1)
                    for j in range(BT):
                        take(k, s, j)
                        at = behind(k, s, j, 2)
                        if at:
                            tanh(*at)
                        at = behind(k, s, j, 4)
                        if at:
                            put_out(at[0], at[1], q - (at[1] > s), at[2])
                ring_blocks(act, body)
                last = (BLOCKS - 1, RING - 1)
                for j in range(BT - 2, BT):
                    tanh(*last, j)
                    put_out(*last, BLOCKS // RING - 1, j - 2)
                for j in range(BT - 2, BT):
                    put_out(*last, BLOCKS // RING - 1, j)

            @block.vector
            def _(v):
                STEPS = 6

                def edges(k, s, q):
                    v.wait_ge(rows_in[s], q * 48 + 48)
                    v.wait_ge(idx_in[s], q * 16 + 16)
                    wait(v, full_done, (k - (RING - 1)) * BT)
                    v.tensor_scalar(spread[:, s, :], rel_b[:, s, :], core.iota_col[0:K, 1 if stack else 0:][:, 0:1],
                                    None, ALU.is_equal).then_inc(spread_done, 1)
                    wait(v, sum_done, (k - (RING - 1)) * BT)
                    v.tensor_tensor(same[:, s, :, :], src_b[:, s, :].rearrange("p (t e) -> p t e", t=BT),
                                    idx[0:ET, s, :].unsqueeze(2).to_broadcast([ET, BT, ET]),
                                    ALU.is_equal).then_inc(same_done, 1)
                    base = k * STEPS
                    wait(v, to_done, k)
                    v.tensor_copy(src_f[:, :], idx[0:ET, s, :]).then_inc(step, 1)
                    v.wait_ge(same_done, k + 1)
                    v.tensor_tensor(earlier[:, :, :], same[:, s, :, :],
                                    before[:, :].unsqueeze(1).to_broadcast([ET, BT, ET]), ALU.mult).then_inc(step, 1)
                    v.wait_ge(step, base + 2)
                    v.tensor_reduce(seen[:, :], earlier[:, :, :], AX_X, ALU.add).then_inc(step, 1)
                    v.tensor_scalar(away[:, :], src_f[:, :], core.iota_col[0:ET, 2:3], -1.0, ALU.subtract,
                                    ALU.mult).then_inc(step, 1)
                    v.wait_ge(step, base + 4)
                    v.tensor_scalar(seen[:, :], seen[:, :], 1.0, None, ALU.min).then_inc(step, 1)
                    v.wait_ge(step, base + 5)
                    v.tensor_tensor(away[:, :], away[:, :], seen[:, :], ALU.mult).then_inc(step, 1)
                    v.wait_ge(step, base + 6)
                    for c in range(COPIES):
                        n = (q - 1) * (RING * BT // COPIES) + ((s + 1) * BT - 1 - c) // COPIES + 1
                        if not isinstance(q, int) or q >= 1:
                            cc = ((s + 1) * BT - 1 - c) % COPIES
                            v.wait_ge(scattered[cc], n * 16)
                    v.tensor_tensor(to_rows[0:ET, s, :], src_f[:, :], away[:, :], ALU.add).then_inc(to_done, 1)

                def basis_sums(k, s, j):
                    v.wait_ge(full_done, k * BT + j + 1)
                    wait(v, i1_done, used(k, j))
                    v.tensor_tensor(prod[:, j % 2, :, 0:NBASIS],
                                    full[j % 2].rearrange("e (c b) -> e c b", b=NBASIS),
                                    basis[:, s, j, :].unsqueeze(1).to_broadcast([ET, D, NBASIS]),
                                    ALU.mult).then_inc(prod_done, 1)
                    v.wait_ge(prod_done, k * BT + j + 1)
                    wait(v, i2_done, used(k, j))
                    v.tensor_reduce(i1[:, j % 2, :], prod[:, j % 2, :, :], AX_X, ALU.add).then_inc(i1_done, 1)

                for i in range(2):
                    v.tensor_copy(prod[:, i, :, NBASIS:NBASIS + 1], core.b_ii[:, :].unsqueeze(2)).then_inc(bias_set, 1)
                v.wait_ge(bias_set, 2)
                v.wait_ge(mask_in, 32)
                edges(0, 0, 0)

                def body(k, s, q):
                    v.wait_ge(rows_in[s], q * 48 + 48)
                    for j in range(BT):
                        basis_sums(k, s, j)
                        if j == 3 and (not isinstance(k, int) or k + 1 < BLOCKS):
                            edges(k + 1, (s + 1) % RING, q + (s + 1) // RING)
                ring_blocks(v, body)


def finish_pairs(core, win):
    nc = core.nc
    with Stage(nc, f"last_{win}") as st:
        got = [st.sb(f"got{i}", [ET, NT, D]) for i in range(COPIES)]
        loaded, step = st.sem("loaded"), st.sem("step")
        with nc.Block() as block:

            @block.sync
            def _(sp):
                for i in range(COPIES):
                    sp.dma_start(got[i][:, :, :], core.sums[i][0:N, :].rearrange("(t p) c -> p t c", p=ET)
                                 ).then_inc(loaded, 16)

            @block.vector
            def _(v):
                v.tensor_tensor(core.x[:, :, :], core.x[:, :, :], core.h[:, :, :], ALU.add).then_inc(step, 1)
                v.wait_ge(loaded, 16 * COPIES)
                for i in range(COPIES):
                    v.wait_ge(step, i + 1)
                    v.tensor_tensor(core.x[:, :, :], core.x[:, :, :], got[i][:, :, :], ALU.add).then_inc(step, 1)
                v.wait_ge(step, COPIES + 1)


def layers(core, win):
    nc = core.nc
    core.sofar = 0
    nodes = NT * ET + FULL

    def narrow_acc(rows):
        return nc.sbuf_tensor(f"acc_{rows}_{win}_{nc.next_id()}", [rows, nodes], F32)

    with nc.sbuf_tensor(f"acc_gat1_{win}", [P, 2, nodes], F32) as acc:
        with nc.sbuf_tensor(f"h_t1_{win}", [D, N], F32) as h_t:
            normalise(core, f"norm1_{win}", h_t)
            node_tables(core, f"tab1_{win}", lambda c, t: h_t[:, t * ET:(t + 1) * ET],
                        [[core.w_gat1[:, side, :]] for side in range(2)], None, WIDE + HEADS,
                        [(0, 0, WIDE + HEADS, 0)], (1, 0, WIDE + HEADS), lambda pool, row: None,
                        lambda row, part: [(node_rows(core.gat1_rows, (0, WIDE + HEADS)), row[:, :, :])]
                        + window_stores(core.gat1_win, part))
        with nc.sbuf_tensor(f"den_gat1_{win}", [HEADS, nodes], F32) as den:
            clear_sums(core, f"clear1_{win}", [acc[:, :, :], den[:, :]])
            edge_pass(core, Pass("gat1", core.gat1_rows, WIDE + HEADS, HEADS, core.att1, core.gat1_win, WIDE,
                                 ((0, P), (P, 2 * P))), win, acc, den)
            finish_gat1(core, win, acc, den)
        node_tables(core, f"tab2_{win}", lambda c, t: acc[:, c, t * ET:(t + 1) * ET],
                    [[core.w_gat2[:, c, :] for c in range(2)]], None, D + 2,
                    [(0, 0, D, 0), (0, D, D + 1, D + 1)], (0, D + 1, 2 * D + 2),
                    lambda pool, row: pool.memset(row[:, :, D:D + 1], 1.0),
                    lambda row, part: [(node_rows(core.gat2_rows, (0, D + 2)), row[:, :, :])]
                    + window_stores(core.gat2_win, part))
    with narrow_acc(D + 1) as acc:
        clear_sums(core, f"clear2_{win}", [acc[:, :]])
        edge_pass(core, Pass("gat2", core.gat2_rows, D + 2, 1, core.att2, core.gat2_win, D + 1), win, acc, None)
        finish_narrow(core, f"fin2_{win}", acc, "mean, bias", None)

    with nc.sbuf_tensor(f"h_t3_{win}", [D, N], F32) as h_t:
        normalise(core, f"norm3_{win}", h_t)
        node_tables(core, f"tab3_{win}", lambda c, t: h_t[:, t * ET:(t + 1) * ET], [[core.w_rel[:, :]]],
                    core.b_rel[0:1, :], D + 2, [(0, 0, 1, D + 1)], (0, 1, 2),
                    lambda pool, row: (pool.memset(row[:, :, D:D + 1], 1.0),
                                       pool.tensor_copy(row[:, :, 0:D], core.h[:, :, :])),
                    lambda row, part: [(node_rows(core.att_rows, (0, D + 2)), row[:, :, :])]
                    + window_stores(core.att_win, part))
    with narrow_acc(D + 1) as acc:
        clear_sums(core, f"clear3_{win}", [acc[:, :]])
        edge_pass(core, Pass("rel", core.att_rows, D + 2, 1, None, core.att_win, D + 1), win, acc, None)
        finish_narrow(core, f"fin3_{win}", acc, "mean, edges", None)

    normalise(core, f"norm4_{win}", None)
    with nc.sbuf_tensor(f"gcn_{win}", [ET, NT, D], F32) as g:
        store_rows(core, f"store_{win}", core.gcn_rows[0], core.h)
        for i, (old, new) in enumerate(((core.h, g), (g, g))):
            with narrow_acc(D) as acc:
                clear_sums(core, f"clear4_{i}_{win}", [acc[:, :]])
                edge_pass(core, Pass(f"gcn{i}", core.gcn_rows[i], D), win, acc, None)
                finish_narrow(core, f"fin4_{i}_{win}", acc, "gcn",
                              {"old": old[:, :, :], "new": g[:, :, :], "last": i == 1},
                              (core.gcn_rows[1].rearrange("(t p) c -> p t c", p=ET), g[:, :, :]) if i == 0 else None)

    with nc.sbuf_tensor(f"h_t5_{win}", [D, N], F32) as h_t:
        normalise(core, f"norm5_{win}", h_t)
        pair_tables(core, win, h_t)
    pair_pass(core, win)
    finish_pairs(core, win)


def store_rows(core, tag, table, rows):
    nc = core.nc
    with Stage(nc, tag) as st:
        stored = st.sem("stored")
        with nc.Block() as block:

            @block.sync
            def _(sp):
                sp.dma_start(table.rearrange("(t p) c -> p t c", p=ET), rows[:, :, :]).then_inc(stored, 16)
                sp.wait_ge(stored, 16)


def gnn_kernel(nc, a, out):
    with ExitStack() as ctx:
        core = Core(nc, ctx, a)
        prepare(core)
        prepare_weights(core)
        span = nc.values_load(core.span[0:1, 0:1], min_val=0, max_val=FULL - 1)
        with nc.If(span < NARROW):
            nc.all_engine_barrier()
            layers(core, NARROW)
        with nc.Else():
            nc.all_engine_barrier()
            layers(core, FULL)
        store_rows(core, "out", out, core.x)


_WEIGHTS = ["L0_gnn_Wl1", "L0_gnn_Wr1", "L0_gnn_att1", "L0_gnn_b1", "L0_gnn_Wl2", "L0_gnn_Wr2", "L0_gnn_att2",
            "L0_gnn_b2", "L1_gnn_head_w", "L1_gnn_head_b", "L1_gnn_tail_w", "L1_gnn_tail_b", "L1_gnn_rel_w",
            "L3_gnn_pp_W", "L3_gnn_pp_b", "L3_gnn_pi_W1", "L3_gnn_pi_b1", "L3_gnn_pi_W2", "L3_gnn_ii_W", "L3_gnn_ii_b"]


def kernel(**inputs):
    import concourse.bacc as _bacc
    from concourse.bass_utils import run_bass_kernel_spmd as _run

    src = np.asarray(inputs["src"])
    src_t = np.zeros((P, TILES), src.dtype)
    src_t[0:ET] = src.reshape(TILES, ET).T
    arrays = {
        "x": inputs["x"], "src": src, "dst": inputs["dst"], "src_t": src_t,
        "dst_t": np.asarray(inputs["dst"]).reshape(TILES, ET).T,
        "next_t": np.roll(np.asarray(inputs["dst"]), -1).reshape(TILES, ET).T,
        "edge_type_t": np.asarray(inputs["edge_type_8"]).reshape(TILES, ET).T,
        "edge_weight_t": np.asarray(inputs["edge_weight"]).reshape(TILES, ET).T,
        "basis_t": np.asarray(inputs["edge_attr_8"]).reshape(TILES, ET, NBASIS).transpose(1, 0, 2).reshape(ET, -1),
    }
    for n in _WEIGHTS:
        arrays[n] = inputs[n]
    p = np.arange(P)
    arrays["ident"] = np.eye(P, dtype=np.float32)
    arrays["iota"] = p.astype(np.float32)
    arrays["iota_cols"] = np.stack([p, p // PARTS, N + p], 1).astype(np.float32)
    arrays["before"] = np.tril(np.ones((ET, ET), np.float32), -1)
    arrays["spare_rows"] = np.repeat((N + p).astype(np.int32)[:, None], RING * BT, 1)
    arrays["head_of"] = np.stack([[(p // D + 2 * c == h) for c in range(2)] for h in range(HEADS)]).astype(np.float32)
    nc = _bacc.Bacc("TRN2", target_bir_lowering=False, num_devices=1)
    arrays = {f"in_{n}": np.ascontiguousarray(v) for n, v in arrays.items()}
    a = {n[3:]: nc.dram_tensor(n, v.shape, mybir.dt.from_np(v.dtype), kind="ExternalInput").ap()
         for n, v in arrays.items()}
    out = nc.dram_tensor("out", (N, D), F32, kind="ExternalOutput").ap()
    gnn_kernel(nc, a, out)
    r = _run(nc, [arrays], core_ids=[0])
    return r.results[0]["out"]
```

```python
from contextlib import ExitStack

import numpy as np

import concourse.bass as bass
from concourse import mybir

F32 = mybir.dt.float32
BF16 = mybir.dt.bfloat16
I32 = mybir.dt.int32
ALU = mybir.AluOpType
ACT = mybir.ActivationFunctionType
AX_X = mybir.AxisListType.X

P = 128
N = 3125
E = 103125
D = 64
HEADS = 4
WIDE = HEADS * D
ET = 125
TILES = E // ET
BT = 5
BLOCKS = TILES // BT
BE = BT * ET
RING = 5
ROWS = 55
NT = N // ET
PADT = 2
NP = (NT + PADT) * ET
PARTS = 3
NARROW, FULL = 32, 128
BIG = 1e30
TINY = 1e-30
SLOPE = 0.2
EPS = 1e-5
NBASIS = 8
COPIES = 5
assert TILES * ET == E and BLOCKS * BT == TILES and BLOCKS % RING == 0 and NT * ET == N and BLOCKS % ROWS == 0
assert BT == 5 and RING * BT % COPIES == 0 and BT >= COPIES
assert 2 * (FULL - 1) < PADT * ET + FULL


class Stage:

    def __init__(self, nc, tag):
        self.nc, self.tag, self.ctx, self.nums = nc, tag, ExitStack(), []

    def sb(self, name, shape, dt=F32):
        return self.ctx.enter_context(self.nc.sbuf_tensor(f"{self.tag}_{name}", shape, dt))

    def bank(self, name, dt=F32):
        words = 512 if dt == F32 else 1024
        return self.ctx.enter_context(self.nc.psum_tensor(f"{self.tag}_ps_{name}", [P, words], dt))

    def sem(self, name):
        s = self.ctx.enter_context(self.nc.semaphore(f"{self.tag}_{name}"))
        self.nums.append(s.num)
        return s

    def __enter__(self):
        return self

    def __exit__(self, *e):
        if e[0] is None and self.nums:
            self.nc.all_engine_barrier(sems_to_clear=range(min(self.nums), max(self.nums) + 1))
        self.ctx.close()
        return False


class Core:

    def __init__(self, nc, ctx, a):
        self.nc, self.a = nc, a

        def sb(name, shape, dt=F32):
            return ctx.enter_context(nc.sbuf_tensor(name, shape, dt))

        self.ident = sb("ident", [P, P])
        self.identb = sb("identb", [P, P], BF16)
        self.iota_row = sb("iota_row", [P, P])
        self.iota_col = sb("iota_col", [P, 3])
        self.ones = sb("ones", [P, P])
        self.zeros = sb("zeros", [ET, D])
        self.x = sb("x", [ET, NT, D])
        self.h = sb("h", [ET, NT, D])
        self.rel = sb("rel", [ET, TILES])
        self.ew = sb("ew", [ET, TILES])
        self.relw = sb("relw", [ET, TILES])
        self.first = sb("first", [1, TILES], I32)
        self.span = sb("span", [1, 1], I32)
        self.times = sb("times", [ET, TILES])
        self.has_edges = sb("has_edges", [ET, NT])
        self.w_gat1 = sb("w_gat1", [D, 2, WIDE + HEADS])
        self.att1 = sb("att1", [P, 2, HEADS])
        self.w_gat2 = sb("w_gat2", [P, 2, 2 * (D + 1)])
        self.att2 = sb("att2", [D + 1, 1])
        self.w_rel = sb("w_rel", [D, 2])
        self.b_rel = sb("b_rel", [1, 2])
        self.b1 = sb("b1", [P, 2])
        self.b2 = sb("b2", [ET, D])
        self.head_of = sb("head_of", [HEADS, 2, P])
        self.w_pp = sb("w_pp", [D, D])
        self.b_pp = sb("b_pp", [D, 1])
        self.w_pair = sb("w_pair", [D, 2, D])
        self.b_pair = sb("b_pair", [1, D])
        self.w_basis = sb("w_basis", [D, D * NBASIS])
        self.w_stack = sb("w_stack", [P, 3, D * NBASIS], BF16)
        self.b_ii = sb("b_ii", [ET, D])

        self.sofar = 0
        self.gathered = [ctx.enter_context(nc.semaphore(f"gathered{s}")) for s in range(RING)]
        self.scattered = [ctx.enter_context(nc.semaphore(f"scattered{c}")) for c in range(COPIES)]

        def dram(name, shape, dt=F32):
            return nc.dram_tensor(name, shape, dt).ap()

        self.rel_row = dram("rel_row", [E], BF16)
        self.reset_row = dram("reset_row", [E + 1], BF16)
        self.gat1_rows = dram("gat1_rows", [N, WIDE + HEADS])
        self.gat1_win = dram("gat1_win", [NP, PARTS, WIDE + HEADS], BF16)
        self.gat2_rows = dram("gat2_rows", [N, D + 2])
        self.gat2_win = dram("gat2_win", [NP, PARTS, D + 1], BF16)
        self.att_rows = dram("att_rows", [N, D + 2])
        self.att_win = dram("att_win", [NP, PARTS, 2], BF16)
        self.gcn_rows = [dram(f"gcn_rows{i}", [N, D]) for i in range(2)]
        self.pair_rows = dram("pair_rows", [N, 4 * D], BF16)
        self.pair_win = dram("pair_win", [NP, PARTS, D * NBASIS], BF16)
        self.sums = [dram(f"sums{i}", [NP, D]) for i in range(COPIES)]


def as_row(v):
    return v.rearrange("(a n) -> a n", a=1)


def prepare(core):
    nc, a = core.nc, core.a
    RE = E // ROWS
    with Stage(nc, "prep") as st:
        dst_t = st.sb("dst_t", [ET, TILES], I32)
        next_t = st.sb("next_t", [ET, TILES], I32)
        type_t = st.sb("type_t", [ET, TILES], I32)
        relw_b = st.sb("relw_b", [ET, NBASIS])
        term = st.sb("term", [ET, TILES])
        dst_n = st.sb("dst_n", [ROWS, RE], I32)
        prev_n = st.sb("prev_n", [ROWS, RE], I32)
        reset_n = st.sb("reset_n", [ROWS, RE + 1], BF16)
        last = st.sb("last", [1, TILES], I32)
        reach = st.sb("reach", [1, BLOCKS])
        top = st.sb("top", [1, 1])
        loaded, stored, prev_set, step = (st.sem(n) for n in ("loaded", "stored", "prev_set", "step"))
        loads = [
            (core.ident[:, :], a["ident"]),
            (core.iota_row[:, :], as_row(a["iota"]).to_broadcast([P, P])),
            (core.iota_col[:, :], a["iota_cols"]),
            (core.x[:, :, :], a["x"].rearrange("(t p) c -> p t c", p=ET)),
            (core.ew[:, :], a["edge_weight_t"]),
            (core.first[:, :], a["dst_t"][0:1, :]),
            (last[:, :], a["dst_t"][ET - 1:ET, :]),
            (dst_t[:, :], a["dst_t"]),
            (next_t[:, :], a["next_t"]),
            (type_t[:, :], a["edge_type_t"]),
            (relw_b[:, :], as_row(a["L1_gnn_rel_w"]).to_broadcast([ET, NBASIS])),
            (dst_n[:, :], a["dst"].rearrange("(k e) -> k e", k=ROWS)),
            (prev_n[1:ROWS, :], a["dst"][RE - 1:E - 1].rearrange("(k e) -> k e", e=RE)),
            (prev_n[0:1, 1:RE], as_row(a["dst"][0:RE - 1])),
        ]
        with nc.Block() as block:

            @block.sync
            def _(sp):
                sp.wait_ge(prev_set, 1)
                for to, of in loads:
                    sp.dma_start(to, of).then_inc(loaded, 16)

            @block.gpsimd
            def _(pool):
                pool.memset(core.ones[:, :], 1.0)
                pool.memset(core.zeros[:, :], 0.0)

            @block.scalar
            def _(act):
                act.wait_ge(step, 4)
                act.dma_start(core.reset_row[0:E].rearrange("(k e) -> k e", k=ROWS), reset_n[:, 0:RE]).then_inc(stored, 16)
                act.dma_start(as_row(core.reset_row[E:E + 1]), reset_n[0:1, RE:RE + 1]).then_inc(stored, 16)
                act.wait_ge(stored, 16 * 2)

            @block.vector
            def _(v):
                v.memset(prev_n[0:1, 0:1], -1).then_inc(prev_set, 1)
                v.wait_ge(loaded, 16 * len(loads))
                v.tensor_copy(core.identb[:, :], core.ident[:, :]).then_inc(step, 1)
                v.memset(reset_n[:, RE:RE + 1], 0.0).then_inc(step, 1)
                v.tensor_tensor(reset_n[:, 0:RE], dst_n[:, :], prev_n[:, :], ALU.not_equal).then_inc(step, 1)
                v.wait_ge(step, 3)
                v.tensor_scalar(reset_n[:, 0:RE], reset_n[:, 0:RE], -BIG, None, ALU.mult).then_inc(step, 1)
                v.tensor_scalar(core.relw[:, :], type_t[:, :], 0.0, relw_b[:, 0:1], ALU.is_equal,
                                ALU.mult).then_inc(step, 1)
                for k in range(1, NBASIS):
                    v.wait_ge(step, 5 + 2 * (k - 1))
                    v.tensor_scalar(term[:, :], type_t[:, :], float(k), relw_b[:, k:k + 1], ALU.is_equal,
                                    ALU.mult).then_inc(step, 1)
                    v.wait_ge(step, 6 + 2 * (k - 1))
                    v.tensor_tensor(core.relw[:, :], core.relw[:, :], term[:, :], ALU.add).then_inc(step, 1)
                n = 5 + 2 * (NBASIS - 1)
                v.tensor_tensor(reach[:, :], last[:, :].rearrange("a (k t) -> a k t", t=BT)[:, :, BT - 1],
                                core.first[:, :].rearrange("a (k t) -> a k t", t=BT)[:, :, 0], ALU.subtract).then_inc(step, 1)
                v.wait_ge(step, n + 1)
                v.tensor_reduce(top[:, :], reach[:, :], AX_X, ALU.max).then_inc(step, 1)
                v.wait_ge(step, n + 2)
                v.tensor_copy(core.span[:, :], top[:, :]).then_inc(step, 1)
                v.tensor_tensor(core.times[:, :], dst_t[:, :], next_t[:, :], ALU.not_equal).then_inc(step, 1)
                v.wait_ge(step, n + 4)
                v.tensor_scalar(core.times[:, :], core.times[:, :], 1.0, None, ALU.add).then_inc(step, 1)
                v.wait_ge(step, n + 5)


def places(core, win):
    nc, a = core.nc, core.a
    group = tiles_in_window(win)
    RE = E // ROWS
    with Stage(nc, f"places_{win}") as st:
        dst_t = st.sb("dst_t", [ET, TILES], I32)
        first_b = st.sb("first_b", [ET, TILES], I32)
        dst_n = st.sb("dst_n", [ROWS, RE], I32)
        rel_n = st.sb("rel_n", [ROWS, RE], BF16)
        loaded, placed, stored = st.sem("loaded"), st.sem("placed"), st.sem("stored")
        with nc.Block() as block:

            @block.sync
            def _(sp):
                sp.dma_start(dst_n[:, :], a["dst"].rearrange("(k e) -> k e", k=ROWS)).then_inc(loaded, 16)
                sp.dma_start(dst_t[:, :], a["dst_t"]).then_inc(loaded, 16)
                sp.dma_start(first_b[:, :], a["dst_t"][0:1, :].to_broadcast([ET, TILES])).then_inc(loaded, 16)
                sp.wait_ge(placed, 1)
                sp.dma_start(core.rel_row.rearrange("(k e) -> k e", k=ROWS), rel_n[:, :]).then_inc(stored, 16)
                sp.wait_ge(stored, 16)

            @block.vector
            def _(v):
                def groups(x, n):
                    return x.rearrange("k (t e) -> k t e", e=n)

                v.wait_ge(loaded, 48)
                dst3 = groups(dst_n[:, :], group * ET)
                v.tensor_tensor(groups(rel_n[:, :], group * ET), dst3, dst3[:, :, 0:1].to_broadcast(dst3.shape),
                                ALU.subtract).then_inc(placed, 1)
                v.tensor_tensor(groups(core.rel[:, :], group), groups(dst_t[:, :], group),
                                groups(first_b[:, :], group)[:, :, 0:1].to_broadcast([ET, TILES // group, group]),
                                ALU.subtract).then_inc(placed, 1)
                v.wait_ge(placed, 2)


def tiles_in_window(win):
    return BT if win == NARROW else 1


def prepare_weights(core):
    nc, a = core.nc, core.a
    with Stage(nc, "weights") as st:
        att_raw = st.sb("att_raw", [P, 2, HEADS])
        att2_raw = st.sb("att2_raw", [D, 1])
        w_pi2 = st.sb("w_pi2", [D, D * NBASIS])
        w_ii = st.sb("w_ii", [D, D])
        turned_w = st.sb("turned_w", [P, 16, P])
        rest = st.sb("rest", [D, D * NBASIS])
        parts = st.sb("parts", [D, PARTS, D * NBASIS], BF16)
        tmp = [st.bank(f"tmp{i}") for i in range(2)]
        loaded, cleared, pe_done, taken, split, stacked = (
            st.sem(n) for n in ("loaded", "cleared", "pe_done", "taken", "split", "stacked"))
        loads = [
            (core.w_gat1[:, 0, 0:WIDE], a["L0_gnn_Wl1"]),
            (core.w_gat1[:, 1, 0:WIDE], a["L0_gnn_Wr1"]),
            (core.w_gat2[:, :, 0:D], a["L0_gnn_Wl2"].rearrange("(c p) n -> p c n", p=P)),
            (core.w_gat2[:, :, D + 1:2 * D + 1], a["L0_gnn_Wr2"].rearrange("(c p) n -> p c n", p=P)),
            (att2_raw[:, :], a["L0_gnn_att2"].rearrange("a c -> c a")),
            (core.w_rel[:, 0:1], a["L1_gnn_head_w"].rearrange("(c a) -> c a", a=1)),
            (core.w_rel[:, 1:2], a["L1_gnn_tail_w"].rearrange("(c a) -> c a", a=1)),
            (core.b_rel[:, 0:1], as_row(a["L1_gnn_head_b"])),
            (core.b_rel[:, 1:2], as_row(a["L1_gnn_tail_b"])),
            (core.b1[:, :], a["L0_gnn_b1"].rearrange("(c p) -> p c", p=P)),
            (core.b2[:, :], as_row(a["L0_gnn_b2"]).to_broadcast([ET, D])),
            (core.head_of[:, :, :], a["head_of"]),
            (core.w_pp[:, :], a["L3_gnn_pp_W"]),
            (core.b_pp[:, :], a["L3_gnn_pp_b"].rearrange("(c a) -> c a", a=1)),
            (core.w_pair[:, :, :], a["L3_gnn_pi_W1"].rearrange("(s c) n -> c s n", c=D)),
            (core.b_pair[:, :], as_row(a["L3_gnn_pi_b1"])),
            (w_pi2[:, :], a["L3_gnn_pi_W2"]),
            (w_ii[:, :], a["L3_gnn_ii_W"]),
            (core.b_ii[:, :], as_row(a["L3_gnn_ii_b"]).to_broadcast([ET, D])),
        ]
        loads += [(att_raw[(h % 2) * D:(h % 2 + 1) * D, h // 2, h:h + 1],
                   a["L0_gnn_att1"][h:h + 1, :].rearrange("a c -> c a")) for h in range(HEADS)]
        pi2 = w_pi2[:, :].rearrange("k (c b) -> k b c", b=NBASIS)
        turns = []
        for side in range(2):
            for c in range(2):
                turns.append((core.w_gat1[:, side, c * P:(c + 1) * P], D, P))
        for side in range(2):
            for c in range(2):
                turns.append((core.w_gat2[:, c, side * (D + 1):side * (D + 1) + D], P, D))
        for b in range(NBASIS):
            turns.append((pi2[:, b, :], D, D))
        products = []
        for side in range(2):
            pairs = [(turned_w[:, 2 * side + c, 0:D], att_raw[:, c, :]) for c in range(2)]
            products.append((pairs, D, HEADS, core.w_gat1[:, side, WIDE:WIDE + HEADS], SLOPE))
        for side in range(2):
            for c in range(2):
                col = side * (D + 1) + D
                products.append(([(turned_w[0:D, 4 + 2 * side + c, :], att2_raw[:, :])], P, 1,
                                 core.w_gat2[:, c, col:col + 1], SLOPE))
        basis = core.w_basis[:, :].rearrange("k (c b) -> k b c", b=NBASIS)
        for b in range(NBASIS):
            products.append(([(turned_w[0:D, 8 + b, 0:D], w_ii[:, :])], D, D, basis[:, b, :], 1.0))
        nt, np_ = len(turns), len(products)
        with nc.Block() as block:

            @block.scalar
            def _(act):
                act.wait_ge(cleared, 1)
                with nc.allow_non_contiguous_dma(reason="vectors of weights to columns"):
                    for to, of in loads[1::2]:
                        act.dma_start(to, of).then_inc(loaded, 16)

            @block.sync
            def _(sp):
                sp.wait_ge(cleared, 1)
                with nc.allow_non_contiguous_dma(reason="vectors of weights to columns"):
                    for to, of in loads[0::2]:
                        sp.dma_start(to, of).then_inc(loaded, 16)
                sp.wait_ge(split, 5)
                for i, (upper, lower) in enumerate(((0, 0), (1, 1), (0, 2))):
                    sp.dma_start(core.w_stack[0:D, i, :], parts[:, upper, :]).then_inc(stacked, 16)
                    sp.dma_start(core.w_stack[D:2 * D, i, :], parts[:, lower, :]).then_inc(stacked, 16)
                sp.wait_ge(stacked, 16 * 6)

            @block.vector
            def _(v):
                v.memset(att_raw[:, :, :], 0.0).then_inc(cleared, 1)
                v.wait_ge(loaded, 16 * len(loads))
                v.tensor_scalar(core.att1[:, :, :], att_raw[:, :, :], 1.0 - SLOPE, None, ALU.mult)
                v.tensor_scalar(core.att2[0:D, :], att2_raw[:, :], 1.0 - SLOPE, None, ALU.mult)
                v.memset(core.att2[D:D + 1, :], 1.0)
                for i, (w, k, m) in enumerate(turns):
                    v.wait_ge(pe_done, i + 1)
                    v.tensor_copy(turned_w[0:m, i, 0:k], tmp[i % 2][0:m, 0:k]).then_inc(taken, 1)
                for i, (_, m, n, to, factor) in enumerate(products):
                    v.wait_ge(pe_done, nt + i + 1)
                    v.tensor_scalar(to, tmp[(nt + i) % 2][0:m, 0:n], factor, None, ALU.mult).then_inc(taken, 1)
                v.wait_ge(taken, nt + np_)
                v.tensor_copy(parts[:, 0, :], core.w_basis[:, :]).then_inc(split, 1)
                v.wait_ge(split, 1)
                v.tensor_tensor(rest[:, :], core.w_basis[:, :], parts[:, 0, :], ALU.subtract).then_inc(split, 1)
                v.wait_ge(split, 2)
                v.tensor_copy(parts[:, 1, :], rest[:, :]).then_inc(split, 1)
                v.wait_ge(split, 3)
                v.tensor_tensor(rest[:, :], rest[:, :], parts[:, 1, :], ALU.subtract).then_inc(split, 1)
                v.wait_ge(split, 4)
                v.tensor_copy(parts[:, 2, :], rest[:, :]).then_inc(split, 1)

            @block.tensor
            def _(pe):
                pe.wait_ge(loaded, 16 * len(loads))
                for i, (w, k, m) in enumerate(turns):
                    if i >= 2:
                        pe.wait_ge(taken, i - 1)
                    pe.transpose(tmp[i % 2][0:m, 0:k], w, core.ident[0:k, 0:k]).then_inc(pe_done, 1)
                pe.wait_ge(taken, nt)
                for i, (pairs, m, n, _, _) in enumerate(products):
                    if i >= 2:
                        pe.wait_ge(taken, nt + i - 1)
                    for j, (left, right) in enumerate(pairs):
                        mm = nc.tensor.matmul(tmp[(nt + i) % 2][0:m, 0:n], left, right, start=(j == 0),
                                              stop=(j == len(pairs) - 1))
                    mm.then_inc(pe_done, 1)


def normalise(core, tag, h_t):
    nc = core.nc
    with Stage(nc, tag) as st:
        mean, var, std, rstd = (st.sb(n, [ET, NT]) for n in ("mean", "var", "std", "rstd"))
        sq = st.sb("sq", [ET, NT, D])
        tp = [st.bank(f"tp{i}")[0:D, :].rearrange("c (t p) -> c t p", p=P) for i in range(2)]
        step, root, normed, turned, taken = (st.sem(n) for n in ("step", "root", "normed", "turned", "taken"))
        groups = [range(g, min(g + 4, NT)) for g in range(0, NT, 4)] if h_t is not None else []
        with nc.Block() as block:

            @block.vector
            def _(v):
                def wide(c):
                    return c[:, :].unsqueeze(2).to_broadcast([ET, NT, D])

                v.tensor_reduce(mean[:, :], core.x[:, :, :], AX_X, ALU.add).then_inc(step, 1)
                v.wait_ge(step, 1)
                v.tensor_scalar(mean[:, :], mean[:, :], 1.0 / D, None, ALU.mult).then_inc(step, 1)
                v.wait_ge(step, 2)
                v.tensor_tensor(core.h[:, :, :], core.x[:, :, :], wide(mean), ALU.subtract).then_inc(step, 1)
                v.wait_ge(step, 3)
                v.tensor_tensor(sq[:, :, :], core.h[:, :, :], core.h[:, :, :], ALU.mult).then_inc(step, 1)
                v.wait_ge(step, 4)
                v.tensor_reduce(var[:, :], sq[:, :, :], AX_X, ALU.add).then_inc(step, 1)
                v.wait_ge(step, 5)
                v.tensor_scalar(var[:, :], var[:, :], 1.0 / D, EPS, ALU.mult, ALU.add).then_inc(step, 1)
                v.wait_ge(root, 1)
                v.reciprocal(rstd[:, :], std[:, :]).then_inc(step, 1)
                v.wait_ge(step, 7)
                v.tensor_tensor(core.h[:, :, :], core.h[:, :, :], wide(rstd), ALU.mult).then_inc(step, 1)
                v.wait_ge(step, 8)
                v.tensor_scalar(core.h[:, :, :], core.h[:, :, :], 0.0, None, ALU.max).then_inc(normed, 1)

            @block.scalar
            def _(act):
                act.wait_ge(step, 6)
                act.activation(std[:, :], var[:, :], ACT.Sqrt).then_inc(root, 1)
                for g, tiles in enumerate(groups):
                    act.wait_ge(turned, g + 1)
                    n = len(tiles) * ET
                    act.copy(h_t[:, tiles[0] * ET:tiles[0] * ET + n].rearrange("c (t p) -> c t p", p=ET),
                             tp[g % 2][:, 0:len(tiles), 0:ET]).then_inc(taken, 1)

            @block.tensor
            def _(pe):
                for g, tiles in enumerate(groups):
                    if g == 0:
                        pe.wait_ge(normed, 1)
                    if g >= 2:
                        pe.wait_ge(taken, g - 1)
                    for i, t in enumerate(tiles):
                        mm = pe.transpose(tp[g % 2][:, i, 0:ET], core.h[:, t, :], core.ident[0:ET, 0:ET])
                    mm.then_inc(turned, 1)


def node_tables(core, tag, lhs, products, bias, width, rows, split, fill, stores):
    nc = core.nc
    with Stage(nc, tag) as st:
        row = st.sb("row", [ET, NT, width]) if width else None
        sr, s0, s1 = split
        sw = max(2, s1 - s0)
        part = st.sb("part", [ET, PARTS, NT + PADT, sw], BF16)
        rest = st.sb("rest", [ET, 2, s1 - s0])
        res = [[st.bank(f"res{i}_{r}")[0:ET, :] for r in range(len(products))] for i in range(2)]
        made, rows_done, hi, mid, taken, rest_done, filled, stored = (
            st.sem(n) for n in ("made", "rows_done", "hi", "mid", "taken", "rest_done", "filled", "stored"))
        out = stores(row, part)
        with nc.Block() as block:

            @block.tensor
            def _(pe):
                for t in range(NT):
                    if t >= 2:
                        pe.wait_ge(rest_done, t - 1)
                        pe.wait_ge(hi, t - 1)
                    for r, weights in enumerate(products):
                        n = weights[0].shape[-1]
                        for c, w in enumerate(weights):
                            mm = pe.matmul(res[t % 2][r][:, 0:n], lhs(c, t), w, start=(c == 0),
                                           stop=(c == len(weights) - 1 and (bias is None or r > 0)))
                        if bias is not None and r == 0:
                            mm = pe.matmul(res[t % 2][r][:, 0:n], core.ones[0:1, 0:ET], bias, start=False, stop=True)
                    mm.then_inc(made, 1)

            @block.scalar
            def _(act):
                for t in range(NT + 1):
                    if t < NT:
                        act.wait_ge(made, t + 1)
                        for (r, c0, c1, at) in rows:
                            act.copy(row[:, t, at:at + c1 - c0], res[t % 2][r][:, c0:c1])
                        act.copy(part[:, 0, t, 0:s1 - s0], res[t % 2][sr][:, s0:s1]).then_inc(hi, 1)
                    if t > 0:
                        act.wait_ge(rest_done, t)
                        act.copy(part[:, 1, t - 1, 0:s1 - s0], rest[:, (t - 1) % 2, :]).then_inc(mid, 1)

            @block.vector
            def _(v):
                for t in range(NT + 1):
                    if t < NT:
                        v.wait_ge(hi, t + 1)
                        if t >= 2:
                            v.wait_ge(taken, t - 1)
                        v.tensor_tensor(rest[:, t % 2, :], res[t % 2][sr][:, s0:s1], part[:, 0, t, 0:s1 - s0],
                                        ALU.subtract).then_inc(rest_done, 1)
                    if t > 0:
                        v.wait_ge(mid, t)
                        v.wait_ge(rest_done, t)
                        v.tensor_tensor(part[:, 2, t - 1, 0:s1 - s0], rest[:, (t - 1) % 2, :], part[:, 1, t - 1, 0:s1 - s0],
                                        ALU.subtract).then_inc(taken, 1)

            @block.gpsimd
            def _(pool):
                fill(pool, row)
                if sw > s1 - s0:
                    pool.memset(part[:, :, 0:NT, s1 - s0:sw], 0.0)
                pool.memset(part[:, :, NT:NT + PADT, :], 0.0).then_inc(filled, 1)


            @block.sync
            def _(sp):
                sp.wait_ge(filled, 1)
                thirds = (0, NT // 3, 2 * NT // 3, NT)
                for lo, hi_ in zip(thirds, thirds[1:]):
                    sp.wait_ge(taken, hi_)
                    sp.wait_ge(mid, hi_)
                    for to, of in out:
                        end = hi_ if hi_ < NT else to.shape[1]
                        sp.dma_start(to[:, lo:end, :], of[:, lo:end, :]).then_inc(stored, 16)
                sp.wait_ge(stored, 16 * 3 * len(out))


def node_rows(table, cols):
    return table.rearrange("(t p) c -> p t c", p=ET)[:, :, cols[0]:cols[1]]


def window_stores(table, part):
    return [(table[:, q, :].rearrange("(t p) c -> p t c", p=ET), part[:, q, :, :]) for q in range(PARTS)]


def load_window(eng, windows, table, at, win):
    if win == NARROW:
        return eng.dma_start(windows[:, 0, :], table.rearrange("n q c -> (n q) c")[bass.ds(at * PARTS, PARTS * win), :])
    return eng.dma_start(windows, table[bass.ds(at, win), :, :])


class Pass:

    def __init__(self, tag, rows, width, heads=0, relu=None, window=None, a_at=0, chunks=((0, D),), table_dt=F32):
        self.tag = tag
        self.rows = rows
        self.width = width
        self.heads = heads
        self.relu = relu
        self.window = window
        self.a_at = a_at
        self.chunks = chunks


def wait(eng, sem, value, met=None):
    if not isinstance(value, int) or value > 0:
        if met is not None and not isinstance(value, int):
            value = eng.compute_val(value)
            eng.wait_ge(met, 16)
        eng.wait_ge(sem, value)


def ring_blocks(eng, body):
    rings = BLOCKS // RING
    for s in range(RING):
        body(s, s, 0)
    with eng.Fori(1, rings - 1) as q:
        for s in range(RING):
            body(q * RING + s, s, q)
    for s in range(RING):
        body((rings - 1) * RING + s, s, rings - 1)


def edge_pass(core, ps_, win, acc, den, side=()):
    nc, a = core.nc, core.a
    H, att = ps_.heads, ps_.heads > 0
    many = H == HEADS
    gat = ps_.relu is not None
    CH = WIDE // P if many else 1
    CW = P if many else D + 1
    stack = win == NARROW
    K = PARTS * win if stack else win
    NPART = 1 if stack else PARTS
    XR = RING if stack else 1
    FW = ps_.window.shape[2] if att else 0
    WA = CW * CH if many else 0
    G = tiles_in_window(win)
    NG = BT // G
    AHEAD = 2 if stack else 1
    AW = acc.shape[0]
    with Stage(nc, f"{ps_.tag}{win}") as st:
        idx = st.sb("idx", [P, RING, BT], I32)
        src_rows = st.sb("src_rows", [P, RING, BT, ps_.width])
        onehot = st.sb("onehot", [ET, BT, win])
        weighted = st.sb("weighted", [ET, BT, max(H, 1), win])
        idx_in = [st.sem(f"idx_in{s}") for s in range(RING)]
        gathered, sofar = core.gathered, core.sofar
        core.sofar += BLOCKS // RING * BT * 16
        onehot_done, weighted_done, agg_done, upd_done, cleared, side_done = (
            st.sem(n) for n in ("onehot_done", "weighted_done", "agg_done", "upd_done", "cleared", "side_done"))
        agg = [st.bank(f"agg{i}") for i in range(2)]
        if att:
            rel_b = st.sb("rel_b", [K, XR, BE], BF16)
            reset = st.sb("reset", [H, XR, BE + 1], BF16)
            windows = st.sb("windows", [K, XR, NG, NPART, FW], BF16)
            spread = st.sb("spread", [K, RING, BE], BF16)
            logit = st.sb("logit", [H, RING, BE])
            fore = st.sb("fore", [H, BE])
            top = st.sb("top", [H, BE])
            carry = st.sb("carry", [H, RING])
            fade_in = st.sb("fade_in", [H, RING])
            fade = st.sb("fade", [H, RING])
            prob = st.sb("prob", [ET, RING, BT, H])
            fade_w = st.sb("fade_w", [P, RING, 4])
            rows_in = [st.sem(f"rows_in{s}") for s in range(RING)]
            win_in = [st.sem(f"win_in{s}") for s in range(XR)]
            (spread_done, e_done, copied, fore_done, top_done, carried, shifted, fade_max, fade_set, faded,
             fade_wide, fade_taken, back_done, prob_done, scaled, base_done) = (
                st.sem(n) for n in ("spread_done", "e_done", "copied", "fore_done", "top_done", "carried", "shifted",
                                    "fade_max", "fade_set", "faded", "fade_wide", "fade_taken", "back_done",
                                    "prob_done", "scaled", "base_done"))
            e_ps = [st.bank(f"e{i}")[0:H, :] for i in range(2)]
            back_ps = st.bank("back")[0:ET, 0:BT * H]
            fade_bank = st.bank("fade")
            fade_ps = fade_bank[:, 0:4]
            den_own = 4 * win + win > 512
            den_ps = [fade_bank[0:H, FULL:FULL + win] if den_own else agg[i][0:H, 4 * win:5 * win] for i in range(2)]
            base = st.sb("base", [ET, RING, BT, H])
        if gat:
            m_ps = [st.bank(f"m{i}")[0:CW, 0:CH * P].rearrange("c (h e) -> c h e", h=CH) for i in range(2)]
            pos = st.sb("pos", [CW, 2, CH, ET])
            m_done, pos_done, counted = st.sem("m_done"), st.sem("pos_done"), st.sem("counted")

        e_groups = [(g, min(g + 4, BT)) for g in range(0, BT, 4)]
        assert len(e_groups) == 2


        with nc.Block() as block:

            @block.sync
            def _(sp):
                def body(k, s, q):
                    wait(sp, gathered[s], sofar + q * (16 * BT))
                    sp.dma_start(idx[:, s, :], a["src_t"][:, bass.ds(k * BT, BT)]).then_inc(idx_in[s], 16)
                    if not att:
                        return
                    wait(sp, spread_done, k - (XR - 1))
                    sp.dma_start(rel_b[:, s % XR, :], as_row(core.rel_row)[:, bass.ds(k * BE, BE)].to_broadcast([K, BE])
                                 ).then_inc(rows_in[s], 16)
                    wait(sp, top_done, k - (XR - 1))
                    sp.dma_start(reset[:, s % XR, :], as_row(core.reset_row)[:, bass.ds(k * BE, BE + 1)].to_broadcast([H, BE + 1])
                                 ).then_inc(rows_in[s], 16)
                    wait(sp, e_done, (k - (XR - 1)) * BT, met=idx_in[s])
                    for g in range(NG):
                        at = sp.value_load(core.first[0:1, bass.ds(k * BT + g * G, 1)], min_val=0, max_val=N - 1)
                        load_window(sp, windows[:, s % XR, g, :, :], ps_.window, at, win).then_inc(win_in[s % XR], 16)

                def first_ring_then_side(k, s, q):
                    body(k, s, q)
                    if isinstance(k, int) and k == RING - 1:
                        for to, of in side:
                            sp.dma_start(to, of).then_inc(side_done, 16)
                ring_blocks(sp, first_ring_then_side)
                if side:
                    sp.wait_ge(side_done, 16 * len(side))

            @block.gpsimd
            def _(pool):
                def body(k, s, q):
                    wait(pool, idx_in[s], q * 16 + 16, met=idx_in[s])
                    for j in range(BT):
                        wait(pool, agg_done, (k - RING) * NG + j // G + 1, met=idx_in[s])
                        pool.indirect_dma_start(src_rows[:, s, j, :], None, ps_.rows,
                                                bass.IndirectOffsetOnAxis(ap=idx[:, s, j:j + 1], axis=0)
                                                ).then_inc(gathered[s], 16)
                ring_blocks(pool, body)

            @block.tensor
            def _(pe):
                def logits(k, s, j):
                    g, i = j // 4, j % 4
                    if i == 0:
                        wait(pe, copied, (k - 1) * len(e_groups) + g + 1)
                    if gat:
                        pe.wait_ge(pos_done, k * BT + j + 1)
                    if many:
                        extra = src_rows[0:ET, s, j, ps_.a_at:ps_.a_at + H]
                    elif not gat:
                        extra = base[:, s, j, :]
                    to = e_ps[g % 2][:, i * ET:(i + 1) * ET]
                    if many or not gat:
                        pe.matmul(to, extra, core.ident[0:ET, 0:ET], start=True, stop=False, is_transpose=True)
                        for w in range(NPART):
                            mm = pe.matmul(to, windows[:, s % XR, j // G, w, WA:WA + H],
                                           spread[:, s, j * ET:(j + 1) * ET], start=False,
                                           stop=(not gat and w == NPART - 1))
                    if gat:
                        for c in range(CH):
                            mm = pe.matmul(to, ps_.relu[:, c, :] if many else ps_.relu[:, :], pos[:, j % 2, c, :],
                                           start=(not many), stop=(c == CH - 1))
                    mm.then_inc(e_done, 1)

                def stage1(k, s, q):
                    wait(pe, gathered[s], sofar + q * (16 * BT) + 16 * BT, met=idx_in[s])
                    n_win = NG * 16
                    if stack:
                        pe.wait_ge(win_in[s], q * n_win + n_win)
                    else:
                        pe.wait_ge(win_in[0], k * n_win + n_win)
                    pe.wait_ge(spread_done, k + 1)
                    if not gat:
                        pe.wait_ge(base_done, k + 1)
                    for j in range(BT):
                        if gat:
                            wait(pe, pos_done, k * BT + (j - 1 if j else 0), met=None if many else idx_in[s])
                            for c in range(CH):
                                to = m_ps[j % 2][:, c, 0:ET]
                                pe.matmul(to, src_rows[0:ET, s, j, ps_.chunks[c][0]:ps_.chunks[c][0] + CW],
                                          core.ident[0:ET, 0:ET], start=True, stop=False, is_transpose=True)
                                for w in range(NPART):
                                    mm = pe.matmul(to, windows[:, s % XR, j // G, w, c * CW:(c + 1) * CW],
                                                   spread[:, s, j * ET:(j + 1) * ET], start=False,
                                                   stop=(w == NPART - 1))
                            mm.then_inc(m_done, 1)
                            if j:
                                logits(k, s, j - 1)
                        else:
                            logits(k, s, j)
                    if gat:
                        logits(k, s, BT - 1)

                def aggregate(k, s):
                    pe.wait_ge(weighted_done, k + 1)
                    for g in range(NG):
                        tiles = range(g * G, (g + 1) * G)
                        slot = (s * NG + g) % 2
                        wait(pe, upd_done, k * NG + g - (0 if s * NG + g == 0 else 1))

                        def sums(to, left, right):
                            for j in tiles:
                                mm = pe.matmul(to, left(j), right(j), start=(j == tiles[0]), stop=(j == tiles[-1]))
                            return mm

                        if many:
                            for c in range(CH):
                                c0 = ps_.chunks[c][0]
                                sums(agg[slot][:, c * 2 * win:(c + 1) * 2 * win],
                                     lambda j: src_rows[0:ET, s, j, c0:c0 + CW], lambda j: weighted[:, j, 2 * c:2 * c + 2, :])
                            if den_own:
                                wait(pe, upd_done, k * NG + g)
                                pe.wait_ge(fade_taken, k + 1)
                            mm = sums(den_ps[slot], lambda j: prob[:, s, j, :], lambda j: onehot[:, j, :])
                        else:
                            mm = sums(agg[slot][0:AW, 0:win], lambda j: src_rows[0:ET, s, j, 0:AW],
                                      lambda j: weighted[:, j, 0, :])
                        mm.then_inc(agg_done, 1)

                def turn_back(k, s):
                    wait(pe, shifted, k + 1, met=idx_in[s])
                    wait(pe, prob_done, k)
                    for j in range(BT):
                        mm = pe.transpose(back_ps[:, j * H:(j + 1) * H], logit[:, s, j * ET:(j + 1) * ET],
                                          core.ident[0:H, 0:H])
                    mm.then_inc(back_done, 1)

                def spread_fade(k, s):
                    pe.wait_ge(faded, k + 1)
                    if many and den_own:
                        wait(pe, upd_done, k * NG)
                    wait(pe, fade_taken, k)
                    if many:
                        for c in range(CH):
                            mm = pe.matmul(fade_ps[:, c:c + 1], core.head_of[:, c, :], fade[:, s:s + 1],
                                           start=True, stop=True)
                    else:
                        mm = pe.matmul(fade_ps[:, 0:1], core.ones[0:1, :], fade[:, s:s + 1], start=True, stop=True)
                    mm.then_inc(fade_wide, 1)

                def body(k, s, q):
                    if att:
                        stage1(k, s, q)
                        if not isinstance(k, int) or k > 0:
                            turn_back(k - 1, (s - 1) % RING)
                        if not isinstance(k, int) or k > 1:
                            aggregate(k - 2, (s - 2) % RING)
                        if not isinstance(k, int) or k > 0:
                            spread_fade(k - 1, (s - 1) % RING)
                    else:
                        pe.wait_ge(gathered[s], sofar + q * (16 * BT) + 16 * BT)
                        aggregate(k, s)
                ring_blocks(pe, body)
                if att:
                    turn_back(BLOCKS - 1, RING - 1)
                    aggregate(BLOCKS - 2, RING - 2)
                    spread_fade(BLOCKS - 1, RING - 1)
                    aggregate(BLOCKS - 1, RING - 1)

            @block.scalar
            def _(act):
                def body(k, s, q):
                    def copy(g):
                        lo, hi = e_groups[g]
                        act.wait_ge(e_done, k * BT + hi)
                        if g == 0:
                            wait(act, back_done, k - (RING - 1))
                        act.copy(logit[:, s, lo * ET:hi * ET], e_ps[g % 2][:, 0:(hi - lo) * ET]).then_inc(copied, 1)

                    nxt = 0
                    if gat:
                        for j in range(BT):
                            act.wait_ge(m_done, k * BT + j + 1)
                            wait(act, e_done, k * BT + (j - 1 if j else 0))
                            if many:
                                act.activation(pos[:, j % 2, :, :], m_ps[j % 2][:, :, 0:ET], ACT.Relu
                                               ).then_inc(pos_done, 1)
                            else:
                                act.activation(pos[0:D, j % 2, :, :], m_ps[j % 2][0:D, :, 0:ET], ACT.Relu)
                                act.copy(pos[D:CW, j % 2, :, :], m_ps[j % 2][D:CW, :, 0:ET]).then_inc(pos_done, 1)
                            if nxt < len(e_groups) and j >= e_groups[nxt][1] + 1:
                                copy(nxt)
                                nxt += 1
                    for g in range(nxt, len(e_groups)):
                        copy(g)
                    if not isinstance(k, int) or k > 0:
                        weights(k - 1, (s - 1) % RING)

                def weights(k, s):
                    act.wait_ge(fade_set, k + 1)
                    wait(act, fade_wide, k - (RING - 1))
                    act.activation(fade[:, s:s + 1], fade_in[:, s:s + 1], ACT.Exp).then_inc(faded, 1)
                    act.wait_ge(back_done, k + 1)
                    wait(act, agg_done, (k - (RING - 1)) * NG)
                    act.activation(prob[:, s, :, :].rearrange("p t h -> p (t h)"), back_ps, ACT.Exp
                                   ).then_inc(prob_done, 1)
                if att:
                    ring_blocks(act, body)
                    weights(BLOCKS - 1, RING - 1)

            @block.vector
            def _(v):
                def first_of(k, g):
                    return v.value_load(core.first[0:1, bass.ds(k * BT + g * G, 1)], min_val=0, max_val=N - 1)

                def update(k, s, g, at):
                    slot = (s * NG + g) % 2
                    if att and g == 0:
                        v.wait_ge(scaled, k + 1)
                    v.wait_ge(agg_done, k * NG + g + 1)
                    wait(v, upd_done, k * NG + g)
                    if many:
                        sums = agg[slot][:, 0:CH * 2 * win].rearrange("p (x j) -> p x j", j=win)
                        for half in range(2):
                            lo = half * D
                            to = acc[lo:lo + D, :, bass.ds(at, win)]
                            v.tensor_tensor(to, to, sums[lo:lo + D, half:half + 3:2, :], ALU.add)
                        to = den[:, bass.ds(at, win)]
                        v.tensor_tensor(to, to, den_ps[slot], ALU.add).then_inc(upd_done, 1)
                    else:
                        to = acc[:, bass.ds(at, win)]
                        v.tensor_tensor(to, to, agg[slot][0:AW, 0:win], ALU.add).then_inc(upd_done, 1)

                def make_onehot(k):
                    if many:
                        wait(v, agg_done, k * NG)
                    wait(v, weighted_done, k)
                    v.tensor_tensor(onehot[:, :, :],
                                    core.iota_row[0:ET, 0:win].unsqueeze(1).to_broadcast([ET, BT, win]),
                                    core.rel[:, bass.ds(k * BT, BT)].unsqueeze(2).to_broadcast([ET, BT, win]),
                                    ALU.is_equal).then_inc(onehot_done, 1)

                def weigh(k, weights):
                    wait(v, agg_done, k * NG)
                    v.wait_ge(onehot_done, k + 1)
                    h = max(H, 1)
                    v.tensor_tensor(weighted[:, :, :, :],
                                    onehot[:, :, :].unsqueeze(2).to_broadcast([ET, BT, h, win]),
                                    weights.unsqueeze(3).to_broadcast([ET, BT, h, win]),
                                    ALU.mult).then_inc(weighted_done, 1)

                def make_spread(k, s, q):
                    v.wait_ge(rows_in[s], q * 32 + 32)
                    wait(v, e_done, (k - (RING - 1)) * BT)
                    v.tensor_scalar(spread[:, s, :], rel_b[:, s % XR, :], core.iota_col[0:K, 1 if stack else 0:][:, 0:1],
                                    None, ALU.is_equal).then_inc(spread_done, 1)

                def make_base(k, s, q):
                    v.wait_ge(gathered[s], sofar + q * (16 * BT) + 16 * BT)
                    v.tensor_tensor(base[:, s, :, 0], src_rows[0:ET, s, :, ps_.a_at],
                                    core.relw[:, bass.ds(k * BT, BT)], ALU.add).then_inc(base_done, 1)

                def ahead(k, s, q):
                    make_spread(k, s, q)
                    if not gat:
                        make_base(k, s, q)

                def weigh_softmax(k, s):
                    make_onehot(k)
                    v.wait_ge(fade_wide, k + 1)
                    v.tensor_copy(fade_w[:, s, 0:CH], fade_ps[:, 0:CH]).then_inc(fade_taken, 1)
                    v.wait_ge(prob_done, k + 1)
                    if gat:
                        v.tensor_tensor(prob[:, s, :, :], prob[:, s, :, :],
                                        core.times[:, bass.ds(k * BT, BT)].unsqueeze(2).to_broadcast([ET, BT, H]),
                                        ALU.mult).then_inc(counted, 1)
                        v.wait_ge(counted, k + 1)
                    weigh(k, prob[:, s, :, :])

                def fade_sums(k, s, at):
                    v.wait_ge(fade_taken, k + 1)
                    wait(v, upd_done, k * NG)
                    if many:
                        for c in range(CH):
                            to = acc[:, c, bass.ds(at, 1)]
                            v.tensor_tensor(to, to, fade_w[:, s, c:c + 1], ALU.mult)
                        to = den[:, bass.ds(at, 1)]
                        v.tensor_tensor(to, to, fade[:, s:s + 1], ALU.mult).then_inc(scaled, 1)
                    else:
                        to = acc[:, bass.ds(at, 1)]
                        v.tensor_tensor(to, to, fade_w[0:AW, s, 0:1], ALU.mult).then_inc(scaled, 1)

                def sums(k, s, groups):
                    for g in groups:
                        at = first_of(k, g)
                        if att and g == 0:
                            fade_sums(k, s, at)
                        update(k, s, g, at)

                def body(k, s, q):
                    inner = not isinstance(k, int)
                    if not att:
                        make_onehot(k)
                        weigh(k, core.ew[:, bass.ds(k * BT, BT)].unsqueeze(2))
                        sums(k, s, range(NG))
                        return

                    def between(third):
                        if inner or k > 1:
                            spots = (range(0, 2), range(2, 4), range(4, BT)) if NG > 1 else ((), (), range(NG))
                            sums(k - 2, (s - 2) % RING, spots[third])

                    if not inner and k == 0:
                        for i in range(AHEAD):
                            ahead(i, i, 0)
                    v.wait_ge(copied, (k + 1) * len(e_groups))
                    v.wait_ge(rows_in[s], q * 32 + 32)
                    if inner or k > 0:
                        v.wait_ge(carried, k)
                    v.tensor_tensor_scan(fore[:, :], reset[:, s % XR, 0:BE], logit[:, s, :],
                                         carry[:, (s - 1) % RING:(s - 1) % RING + 1] if inner or k > 0 else -BIG,
                                         ALU.add, ALU.max).then_inc(fore_done, 1)
                    between(0)
                    v.wait_ge(fore_done, k + 1)
                    v.tensor_copy(carry[:, s:s + 1], fore[:, BE - 1:BE]).then_inc(carried, 1)
                    v.tensor_tensor_scan(top[:, ::-1], reset[:, s % XR, BE:0:-1], fore[:, ::-1], -BIG,
                                         ALU.add, ALU.max).then_inc(top_done, 1)
                    between(1)
                    v.wait_ge(top_done, k + 1)
                    v.tensor_tensor(logit[:, s, :], logit[:, s, :], top[:, :], ALU.subtract).then_inc(shifted, 1)
                    if inner or k > 0:
                        v.tensor_tensor(fade_in[:, s:s + 1], carry[:, (s - 1) % RING:(s - 1) % RING + 1], top[:, 0:1],
                                        ALU.subtract).then_inc(fade_max, 1)
                    else:
                        v.memset(fade_in[:, s:s + 1], 0.0).then_inc(fade_max, 1)
                    v.wait_ge(fade_max, k + 1)
                    v.tensor_scalar(fade_in[:, s:s + 1], fade_in[:, s:s + 1], 0.0, None, ALU.min).then_inc(fade_set, 1)
                    between(2)
                    if inner or k + AHEAD < BLOCKS:
                        ahead(k + AHEAD, (s + AHEAD) % RING, q + (s + AHEAD) // RING)
                    if inner or k > 0:
                        weigh_softmax(k - 1, (s - 1) % RING)
                accumulators = [acc[:, :, :], den[:, :]] if many else [acc[:, :]]
                for t in accumulators:
                    v.memset(t, 0.0).then_inc(cleared, 1)
                v.wait_ge(cleared, len(accumulators))
                ring_blocks(v, body)
                if att:
                    sums(BLOCKS - 2, RING - 2, range(NG))
                    weigh_softmax(BLOCKS - 1, RING - 1)
                    sums(BLOCKS - 1, RING - 1, range(NG))


def finish_gat1(core, win, acc, den):
    nc = core.nc
    STEP = 4 * ET
    columns = [(n, min(n + STEP, N)) for n in range(0, N, STEP)]
    pieces = [(c, lo, hi) for lo, hi in columns for c in range(2)]
    with Stage(nc, f"fin1_{win}") as st:
        wide = [st.bank(f"wide{i}") for i in range(2)]
        inverted, spread, divided, out = (st.sem(n) for n in ("inverted", "spread", "divided", "out"))
        with nc.Block() as block:

            @block.tensor
            def _(pe):
                for i, (c, lo, hi) in enumerate(pieces):
                    pe.wait_ge(inverted, 2 * (i // 2 + 1))
                    if i >= 2:
                        pe.wait_ge(divided, i - 1)
                    pe.matmul(wide[i % 2][:, 0:hi - lo], core.head_of[:, c, :], den[:, lo:hi], start=True,
                              stop=True).then_inc(spread, 1)

            @block.vector
            def _(v):
                for n in range(len(columns) + 1):
                    if n < len(columns):
                        lo, hi = columns[n]
                        v.tensor_scalar(den[:, lo:hi], den[:, lo:hi], TINY, None, ALU.max).then_inc(inverted, 1)
                        v.wait_ge(inverted, 2 * n + 1)
                        v.reciprocal(den[:, lo:hi], den[:, lo:hi]).then_inc(inverted, 1)
                    for i in range(2 * (n - 1), 2 * n) if n > 0 else ():
                        c, lo, hi = pieces[i]
                        v.wait_ge(spread, i + 1)
                        v.tensor_tensor(acc[:, c, lo:hi], acc[:, c, lo:hi], wide[i % 2][:, 0:hi - lo],
                                        ALU.mult).then_inc(divided, 1)

            @block.scalar
            def _(act):
                for i, (c, lo, hi) in enumerate(pieces):
                    act.wait_ge(divided, i + 1)
                    act.activation(acc[:, c, lo:hi], acc[:, c, lo:hi], ACT.Gelu, bias=core.b1[:, c:c + 1]).then_inc(out, 1)


def finish_narrow(core, tag, acc, kind, g, store=None):
    nc = core.nc
    AW = acc.shape[0]
    groups = [range(n, min(n + 7, NT)) for n in range(0, NT, 7)]
    with Stage(nc, tag) as st:
        back = [st.bank(f"back{i}")[0:ET, :] for i in range(2)]
        mean = st.sb("mean", [ET, NT, D])
        inv = st.sb("inv", [ET, NT])
        turned, step, taken, stored = (st.sem(n) for n in ("turned", "step", "taken", "stored"))
        with nc.Block() as block:

            @block.tensor
            def _(pe):
                for n, tiles in enumerate(groups):
                    if n >= 2:
                        pe.wait_ge(taken, n - 1)
                    for i, t in enumerate(tiles):
                        mm = pe.transpose(back[n % 2][:, i * AW:(i + 1) * AW], acc[:, t * ET:(t + 1) * ET],
                                          core.ident[0:AW, 0:AW])
                    mm.then_inc(turned, 1)

            @block.vector
            def _(v):
                count = [0]

                def then(ins):
                    count[0] += 1
                    ins.then_inc(step, 1)
                    v.wait_ge(step, count[0])

                for n, tiles in enumerate(groups):
                    t0, t1 = tiles[0], tiles[-1] + 1
                    w = t1 - t0
                    b3 = back[n % 2][:, 0:w * AW].rearrange("p (t c) -> p t c", c=AW)
                    v.wait_ge(turned, n + 1)
                    if kind == "gcn":
                        v.tensor_copy(mean[:, t0:t1, :], b3[:, :, 0:D]).then_inc(taken, 1)
                    else:
                        cnt = b3[:, :, AW - 1]
                        if kind == "mean, edges":
                            then(v.tensor_scalar(core.has_edges[:, t0:t1], cnt, 0.0, None, ALU.is_gt))
                        then(v.tensor_scalar(inv[:, t0:t1], cnt, TINY, None, ALU.max))
                        then(v.reciprocal(inv[:, t0:t1], inv[:, t0:t1]))
                        v.tensor_tensor(mean[:, t0:t1, :], b3[:, :, 0:D],
                                        inv[:, t0:t1].unsqueeze(2).to_broadcast([ET, w, D]), ALU.mult).then_inc(taken, 1)
                v.wait_ge(taken, len(groups))
                if kind == "gcn":
                    last = g["last"]
                    old, new = g["old"], g["new"]
                    then(v.tensor_tensor(mean[:, :, :], mean[:, :, :], old, ALU.subtract))
                    then(v.tensor_tensor(mean[:, :, :], mean[:, :, :],
                                         core.has_edges[:, :].unsqueeze(2).to_broadcast([ET, NT, D]), ALU.mult))
                    then(v.tensor_scalar(mean[:, :, :], mean[:, :, :], 0.5, None, ALU.mult))
                    then(v.tensor_tensor(new, mean[:, :, :], old, ALU.add))
                    if last:
                        then(v.tensor_tensor(core.x[:, :, :], core.x[:, :, :], new, ALU.add))
                else:
                    if kind == "mean, bias":
                        then(v.tensor_tensor(mean[:, :, :], mean[:, :, :],
                                             core.b2[:, :].unsqueeze(1).to_broadcast([ET, NT, D]), ALU.add))
                    then(v.tensor_tensor(core.x[:, :, :], core.x[:, :, :], mean[:, :, :], ALU.add))

            if store is not None:
                @block.sync
                def _(sp):
                    sp.wait_ge(step, 4)
                    sp.dma_start(store[0], store[1]).then_inc(stored, 16)
                    sp.wait_ge(stored, 16)


def pair_tables(core, win, h_t):
    nc = core.nc
    STEP = 4 * ET
    pieces = [(n, min(n + STEP, N)) for n in range(0, N, STEP)]
    with ExitStack() as ctx:
        p1 = ctx.enter_context(nc.sbuf_tensor(f"pair_p1_{win}", [D, N], F32))
        v_t = ctx.enter_context(nc.sbuf_tensor(f"pair_v_{win}", [D, N], F32))
        with Stage(nc, f"pair_{win}") as st:
            ps = [st.bank(f"p{i}")[0:D, :] for i in range(2)]
            made, taken = st.sem("made"), st.sem("taken")
            with nc.Block() as block:

                @block.tensor
                def _(pe):
                    m = len(pieces)
                    for i, (w, src, (lo, hi)) in enumerate([(core.w_pp[:, :], h_t, p) for p in pieces]
                                                           + [(core.w_pair[:, 1, :], p1, p) for p in pieces]):
                        if i >= 2:
                            pe.wait_ge(taken, i - 1)
                        if i >= m:
                            pe.wait_ge(taken, i - m + 1)
                        pe.matmul(ps[i % 2][:, 0:hi - lo], w, src[:, lo:hi], start=True, stop=True).then_inc(made, 1)

                @block.scalar
                def _(act):
                    for i, (lo, hi) in enumerate(pieces):
                        act.wait_ge(made, i + 1)
                        act.activation(p1[:, lo:hi], ps[i % 2][:, 0:hi - lo], ACT.Tanh, bias=core.b_pp[:, 0:1]
                                       ).then_inc(taken, 1)
                    for i, (lo, hi) in enumerate(pieces):
                        act.wait_ge(made, len(pieces) + i + 1)
                        act.copy(v_t[:, lo:hi], ps[(len(pieces) + i) % 2][:, 0:hi - lo]).then_inc(taken, 1)
        node_tables(core, f"pair_u_{win}", lambda c, t: p1[:, t * ET:(t + 1) * ET], [[core.w_pair[:, 0, :]]],
                    core.b_pair[0:1, :], 0, [], (0, 0, D), lambda pool, row: None,
                    lambda row, part: [(node_rows(core.pair_rows, (i * D, (i + 1) * D)), part[:, q, 0:NT, :])
                                       for i, q in enumerate((0, 1, 2, 0))])
        node_tables(core, f"pair_w_{win}", lambda c, t: v_t[:, t * ET:(t + 1) * ET], [[core.w_basis[:, :]]],
                    None, 0, [], (0, 0, D * NBASIS), lambda pool, row: None,
                    lambda row, part: window_stores(core.pair_win, part))


def pair_pass(core, win):
    nc, a = core.nc, core.a
    stack = win == NARROW
    K = PARTS * win if stack else win
    NPART = 1 if stack else PARTS
    XR = RING if stack else 1
    G = tiles_in_window(win)
    NG = BT // G
    DB = D * NBASIS
    with Stage(nc, f"pairs{win}") as st:
        idx = st.sb("idx", [P, RING, BT], I32)
        src_rows = st.sb("src_rows", [P, RING, BT, 4 * D], BF16)
        rel_b = st.sb("rel_b", [K, RING, BE], BF16)
        windows = st.sb("windows", [K, XR, NG, NPART, DB], BF16)
        spread = st.sb("spread", [K, RING, BE], BF16)
        basis = st.sb("basis", [ET, RING, BT, NBASIS])
        src_b = st.sb("src_b", [ET, RING, BE], I32)
        same = st.sb("same", [ET, RING, BT, ET])
        earlier = st.sb("earlier", [ET, BT, ET])
        before = st.sb("before", [ET, ET])
        seen = st.sb("seen", [ET, BT])
        src_f = st.sb("src_f", [ET, BT])
        away = st.sb("away", [ET, BT])
        to_rows = st.sb("to_rows", [P, RING, BT], I32)
        hid = st.sb("hid", [P, 2, 2, ET], BF16)
        prod = st.sb("prod", [ET, 2, D, NBASIS + 1])
        i1 = st.sb("i1", [ET, 2, D])
        i2 = st.sb("i2", [ET, 2, D])
        out = st.sb("out", [P, COPIES, D])
        idx_in = [st.sem(f"idx_in{s}") for s in range(RING)]
        rows_in = [st.sem(f"rows_in{s}") for s in range(RING)]
        gathered, sofar = core.gathered, core.sofar
        core.sofar += BLOCKS // RING * BT * 16
        win_in = [st.sem(f"win_in{s}") for s in range(XR)]
        scattered = core.scattered
        (spread_done, same_done, to_done, set_up, turned, hid_done, full_done, prod_done, i1_done,
         i2_done, sum_done, out_done, mask_in, step, bias_set) = (
            st.sem(n) for n in ("spread_done", "same_done", "to_done", "set_up", "turned", "hid_done",
                                "full_done", "prod_done", "i1_done", "i2_done", "sum_done", "out_done", "mask_in",
                                "step", "bias_set"))
        turn_ps = [st.bank(f"turn{i}", BF16)[:, 0:2 * P].rearrange("p (h e) -> p h e", h=2) for i in range(2)]
        full = [st.bank(f"full{i}")[0:ET, :] for i in range(2)]
        sum_ps = [st.bank(f"sum{i}")[0:ET, 0:D] for i in range(2)]
        TANH_LAG, SUM_LAG, SCATTER_LAG = 1, 3, 5


        def used(k, j):
            return k * BT + (j - 1 if j else 0)

        def behind(k, s, j, lag):
            if j >= lag:
                return k, s, j - lag
            if isinstance(k, int) and k == 0:
                return None
            return k - 1, (s - 1) % RING, j - lag + BT

        with nc.Block() as block:

            @block.sync
            def _(sp):
                sp.dma_start(before[:, :], a["before"]).then_inc(mask_in, 16)
                sp.dma_start(to_rows[:, :, :].rearrange("p r t -> p (r t)"), a["spare_rows"]).then_inc(mask_in, 16)

                def body(k, s, q):
                    wait(sp, gathered[s], sofar + q * (16 * BT), met=idx_in[s])
                    wait(sp, to_done, k - (RING - 1), met=idx_in[s])
                    sp.dma_start(idx[:, s, :], a["src_t"][:, bass.ds(k * BT, BT)]).then_inc(idx_in[s], 16)
                    wait(sp, spread_done, k - (RING - 1))
                    sp.dma_start(rel_b[:, s, :], as_row(core.rel_row)[:, bass.ds(k * BE, BE)].to_broadcast([K, BE])
                                 ).then_inc(rows_in[s], 16)
                    wait(sp, same_done, k - (RING - 1), met=idx_in[s])
                    sp.dma_start(src_b[:, s, :], a["src"].rearrange("(k e) -> k e", k=BLOCKS)[bass.ds(k, 1), :]
                                 .to_broadcast([ET, BE])).then_inc(rows_in[s], 16)
                    wait(sp, prod_done, (k - (RING - 1)) * BT)
                    sp.dma_start(basis[:, s, :, :].rearrange("p t b -> p (t b)"),
                                 a["basis_t"][:, bass.ds(k * (BT * NBASIS), BT * NBASIS)]).then_inc(rows_in[s], 16)
                    wait(sp, full_done, (k - (XR - 1)) * BT, met=idx_in[s])
                    for g in range(NG):
                        at = sp.value_load(core.first[0:1, bass.ds(k * BT + g * G, 1)], min_val=0, max_val=N - 1)
                        load_window(sp, windows[:, s % XR, g, :, :], core.pair_win, at, win).then_inc(win_in[s % XR], 16)
                ring_blocks(sp, body)

            @block.gpsimd
            def _(pool):
                pool.memset(out[:, :, :], 0.0).then_inc(set_up, 1)
                pool.wait_ge(mask_in, 32)

                def gather(k, s, q, j):
                    if j == 0:
                        wait(pool, idx_in[s], q * 16 + 16, met=idx_in[s])
                    wait(pool, turned, (k - RING) * BT + j + 1, met=idx_in[s])
                    pool.indirect_dma_start(src_rows[:, s, j, :], None, core.pair_rows,
                                            bass.IndirectOffsetOnAxis(ap=idx[:, s, j:j + 1], axis=0)
                                            ).then_inc(gathered[s], 16)

                def scatter(k, s, q, j):
                    c, n = (s * BT + j) % COPIES, q * (RING * BT // COPIES) + (s * BT + j) // COPIES
                    if j == 0:
                        wait(pool, to_done, k + 1, met=idx_in[s])
                    wait(pool, out_done, k * BT + j + 1, met=idx_in[s])
                    wait(pool, scattered[c], n * 16, met=idx_in[s])
                    pool.indirect_dma_start(core.sums[c], bass.IndirectOffsetOnAxis(ap=to_rows[:, s, j:j + 1], axis=0),
                                            out[:, c, :], None, bounds_check=NP - 1, oob_is_err=True,
                                            compute_op=ALU.add).then_inc(scattered[c], 16)

                for j in range(BT):
                    gather(0, 0, 0, j)

                def body(k, s, q):
                    for j in range(BT):
                        if not isinstance(k, int) or k + 1 < BLOCKS:
                            gather(k + 1, (s + 1) % RING, q + (s + 1) // RING, j)
                        at = behind(k, s, j, SCATTER_LAG)
                        if at:
                            scatter(at[0], at[1], q - (at[1] > s), at[2])
                ring_blocks(pool, body)
                for j in range(BT - SCATTER_LAG, BT):
                    scatter(BLOCKS - 1, RING - 1, BLOCKS // RING - 1, j)
                for c in range(COPIES):
                    pool.wait_ge(scattered[c], 16 * (TILES // COPIES))

            @block.tensor
            def _(pe):
                def turn(k, s, q, j):
                    if j == 0:
                        pe.wait_ge(gathered[s], sofar + q * (16 * BT) + 16 * BT)
                    wait(pe, hid_done, used(k, j))
                    for h in range(2):
                        mm = pe.transpose(turn_ps[j % 2][:, h, 0:ET], src_rows[0:ET, s, j, h * P:(h + 1) * P],
                                          core.identb[0:ET, 0:ET])
                    mm.then_inc(turned, 1)

                def expand(k, s, q, j):
                    if j == 0:
                        pe.wait_ge(spread_done, k + 1)
                        n_win = NG * 16
                        if stack:
                            pe.wait_ge(win_in[s], q * n_win + n_win)
                        else:
                            pe.wait_ge(win_in[0], k * n_win + n_win)
                    pe.wait_ge(hid_done, k * BT + j + 1)
                    wait(pe, prod_done, used(k, j))
                    to = full[j % 2]
                    for i, h in enumerate((0, 0, 1)):
                        pe.matmul(to, hid[:, j % 2, h, :], core.w_stack[:, i, :], start=(i == 0), stop=False)
                    for w in range(NPART):
                        mm = pe.matmul(to, spread[:, s, j * ET:(j + 1) * ET], windows[:, s % XR, j // G, w, :],
                                       start=False, stop=(w == NPART - 1))
                    mm.then_inc(full_done, 1)

                def sum_same(k, s, j):
                    if j == 0:
                        pe.wait_ge(same_done, k + 1)
                    pe.wait_ge(i2_done, k * BT + j + 1)
                    wait(pe, out_done, used(k, j))
                    pe.matmul(sum_ps[j % 2], same[:, s, j, :], i2[:, j % 2, :], start=True, stop=True
                              ).then_inc(sum_done, 1)

                def body(k, s, q):
                    for j in range(BT):
                        turn(k, s, q, j)
                        at = behind(k, s, j, TANH_LAG)
                        if at:
                            expand(at[0], at[1], q - (at[1] > s), at[2])
                        at = behind(k, s, j, SUM_LAG)
                        if at:
                            sum_same(*at)
                ring_blocks(pe, body)
                expand(BLOCKS - 1, RING - 1, BLOCKS // RING - 1, BT - 1)
                for j in range(BT - SUM_LAG, BT):
                    sum_same(BLOCKS - 1, RING - 1, j)

            @block.scalar
            def _(act):
                def take(k, s, j):
                    act.wait_ge(turned, k * BT + j + 1)
                    wait(act, full_done, used(k, j))
                    act.copy(hid[:, j % 2, :, :], turn_ps[j % 2][:, :, 0:ET]).then_inc(hid_done, 1)

                def tanh(k, s, j):
                    act.wait_ge(i1_done, k * BT + j + 1)
                    wait(act, sum_done, used(k, j))
                    act.activation(i2[:, j % 2, :], i1[:, j % 2, :], ACT.Tanh).then_inc(i2_done, 1)

                def put_out(k, s, q, j):
                    c, n = (s * BT + j) % COPIES, q * (RING * BT // COPIES) + (s * BT + j) // COPIES
                    act.wait_ge(sum_done, k * BT + j + 1)
                    wait(act, scattered[c], n * 16)
                    act.copy(out[0:ET, c, :], sum_ps[j % 2]).then_inc(out_done, 1)

                def body(k, s, q):
                    if isinstance(k, int) and k == 0:
                        act.wait_ge(set_up, 1)
                    for j in range(BT):
                        take(k, s, j)
                        at = behind(k, s, j, 2)
                        if at:
                            tanh(*at)
                        at = behind(k, s, j, 4)
                        if at:
                            put_out(at[0], at[1], q - (at[1] > s), at[2])
                ring_blocks(act, body)
                last = (BLOCKS - 1, RING - 1)
                for j in range(BT - 2, BT):
                    tanh(*last, j)
                    put_out(*last, BLOCKS // RING - 1, j - 2)
                for j in range(BT - 2, BT):
                    put_out(*last, BLOCKS // RING - 1, j)

            @block.vector
            def _(v):
                STEPS = 5

                def edges(k, s, q, part):
                    base = k * STEPS
                    if part == 0:
                        v.wait_ge(rows_in[s], q * 48 + 48)
                        v.wait_ge(idx_in[s], q * 16 + 16)
                        wait(v, full_done, (k - (RING - 1)) * BT)
                        v.tensor_scalar(spread[:, s, :], rel_b[:, s, :], core.iota_col[0:K, 1 if stack else 0:][:, 0:1],
                                        None, ALU.is_equal).then_inc(spread_done, 1)
                        wait(v, to_done, k)
                        v.tensor_copy(src_f[:, :], idx[0:ET, s, :]).then_inc(step, 1)
                    elif part == 1:
                        wait(v, sum_done, (k - (RING - 1)) * BT)
                        v.tensor_tensor(same[:, s, :, :], src_b[:, s, :].rearrange("p (t e) -> p t e", t=BT),
                                        idx[0:ET, s, :].unsqueeze(2).to_broadcast([ET, BT, ET]),
                                        ALU.is_equal).then_inc(same_done, 1)
                        v.wait_ge(step, base + 1)
                        v.tensor_scalar(away[:, :], src_f[:, :], core.iota_col[0:ET, 2:3], -1.0, ALU.subtract,
                                        ALU.mult).then_inc(step, 1)
                    elif part == 2:
                        v.wait_ge(same_done, k + 1)
                        v.tensor_tensor(earlier[:, :, :], same[:, s, :, :],
                                        before[:, :].unsqueeze(1).to_broadcast([ET, BT, ET]), ALU.mult).then_inc(step, 1)
                    elif part == 3:
                        v.wait_ge(step, base + 3)
                        v.tensor_reduce(seen[:, :], earlier[:, :, :], AX_X, ALU.add).then_inc(step, 1)
                    else:
                        v.wait_ge(step, base + 4)
                        v.scalar_tensor_tensor(away[:, :], seen[:, :], 1.0, away[:, :], ALU.min, ALU.mult
                                               ).then_inc(step, 1)
                        v.wait_ge(step, base + 5)
                        for c in range(COPIES):
                            n = (q - 1) * (RING * BT // COPIES) + ((s + 1) * BT - 1 - c) // COPIES + 1
                            if not isinstance(q, int) or q >= 1:
                                v.wait_ge(scattered[((s + 1) * BT - 1 - c) % COPIES], n * 16)
                        v.tensor_tensor(to_rows[0:ET, s, :], src_f[:, :], away[:, :], ALU.add).then_inc(to_done, 1)

                def basis_sums(k, s, j):
                    v.wait_ge(full_done, k * BT + j + 1)
                    wait(v, i1_done, used(k, j))
                    v.tensor_tensor(prod[:, j % 2, :, 0:NBASIS],
                                    full[j % 2].rearrange("e (c b) -> e c b", b=NBASIS),
                                    basis[:, s, j, :].unsqueeze(1).to_broadcast([ET, D, NBASIS]),
                                    ALU.mult).then_inc(prod_done, 1)
                    v.wait_ge(prod_done, k * BT + j + 1)
                    wait(v, i2_done, used(k, j))
                    v.tensor_reduce(i1[:, j % 2, :], prod[:, j % 2, :, :], AX_X, ALU.add).then_inc(i1_done, 1)

                for i in range(2):
                    v.tensor_copy(prod[:, i, :, NBASIS:NBASIS + 1], core.b_ii[:, :].unsqueeze(2)).then_inc(bias_set, 1)
                v.wait_ge(bias_set, 2)
                v.wait_ge(mask_in, 32)
                for part in range(BT):
                    edges(0, 0, 0, part)

                def body(k, s, q):
                    v.wait_ge(rows_in[s], q * 48 + 48)
                    for j in range(BT):
                        basis_sums(k, s, j)
                        if not isinstance(k, int) or k + 1 < BLOCKS:
                            edges(k + 1, (s + 1) % RING, q + (s + 1) // RING, j)
                ring_blocks(v, body)


def finish_pairs(core, win):
    nc = core.nc
    with Stage(nc, f"last_{win}") as st:
        got = [st.sb(f"got{i}", [ET, NT, D]) for i in range(COPIES)]
        loaded, step = [st.sem(f"loaded{i}") for i in range(COPIES)], st.sem("step")
        with nc.Block() as block:

            @block.sync
            def _(sp):
                for i in range(COPIES):
                    sp.dma_start(got[i][:, :, :], core.sums[i][0:N, :].rearrange("(t p) c -> p t c", p=ET)
                                 ).then_inc(loaded[i], 16)

            @block.vector
            def _(v):
                v.tensor_tensor(core.x[:, :, :], core.x[:, :, :], core.h[:, :, :], ALU.add).then_inc(step, 1)
                for i in range(COPIES):
                    v.wait_ge(loaded[i], 16)
                    v.wait_ge(step, i + 1)
                    v.tensor_tensor(core.x[:, :, :], core.x[:, :, :], got[i][:, :, :], ALU.add).then_inc(step, 1)
                v.wait_ge(step, COPIES + 1)


def layers(core, win):
    nc = core.nc
    core.sofar = 0
    places(core, win)
    nodes = NT * ET + FULL

    def narrow_acc(rows):
        return nc.sbuf_tensor(f"acc_{rows}_{win}_{nc.next_id()}", [rows, nodes], F32)

    with nc.sbuf_tensor(f"acc_gat1_{win}", [P, 2, nodes], F32) as acc:
        with nc.sbuf_tensor(f"h_t1_{win}", [D, N], F32) as h_t:
            normalise(core, f"norm1_{win}", h_t)
            node_tables(core, f"tab1_{win}", lambda c, t: h_t[:, t * ET:(t + 1) * ET],
                        [[core.w_gat1[:, side, :]] for side in range(2)], None, WIDE + HEADS,
                        [(0, 0, WIDE + HEADS, 0)], (1, 0, WIDE + HEADS), lambda pool, row: None,
                        lambda row, part: [(node_rows(core.gat1_rows, (0, WIDE + HEADS)), row[:, :, :])]
                        + window_stores(core.gat1_win, part))
        with nc.sbuf_tensor(f"den_gat1_{win}", [HEADS, nodes], F32) as den:
            edge_pass(core, Pass("gat1", core.gat1_rows, WIDE + HEADS, HEADS, core.att1, core.gat1_win, WIDE,
                                 ((0, P), (P, 2 * P))), win, acc, den)
            finish_gat1(core, win, acc, den)
        node_tables(core, f"tab2_{win}", lambda c, t: acc[:, c, t * ET:(t + 1) * ET],
                    [[core.w_gat2[:, c, :] for c in range(2)]], None, D + 2,
                    [(0, 0, D + 1, 0)], (0, D + 1, 2 * D + 2),
                    lambda pool, row: pool.memset(row[:, :, D + 1:D + 2], 1.0),
                    lambda row, part: [(node_rows(core.gat2_rows, (0, D + 2)), row[:, :, :])]
                    + window_stores(core.gat2_win, part))
    with narrow_acc(D + 2) as acc:
        edge_pass(core, Pass("gat2", core.gat2_rows, D + 2, 1, core.att2, core.gat2_win), win, acc, None)
        finish_narrow(core, f"fin2_{win}", acc, "mean, bias", None)

    with nc.sbuf_tensor(f"h_t3_{win}", [D, N], F32) as h_t:
        normalise(core, f"norm3_{win}", h_t)
        node_tables(core, f"tab3_{win}", lambda c, t: h_t[:, t * ET:(t + 1) * ET], [[core.w_rel[:, :]]],
                    core.b_rel[0:1, :], D + 2, [(0, 0, 1, D + 1)], (0, 1, 2),
                    lambda pool, row: (pool.memset(row[:, :, D:D + 1], 1.0),
                                       pool.tensor_copy(row[:, :, 0:D], core.h[:, :, :])),
                    lambda row, part: [(node_rows(core.att_rows, (0, D + 2)), row[:, :, :])]
                    + window_stores(core.att_win, part))
    with narrow_acc(D + 1) as acc:
        edge_pass(core, Pass("rel", core.att_rows, D + 2, 1, None, core.att_win, D + 1), win, acc, None)
        finish_narrow(core, f"fin3_{win}", acc, "mean, edges", None)

    normalise(core, f"norm4_{win}", None)
    with nc.sbuf_tensor(f"gcn_{win}", [ET, NT, D], F32) as g:
        store_rows(core, f"store_{win}", core.gcn_rows[0], core.h)
        for i, (old, new) in enumerate(((core.h, g), (g, g))):
            with narrow_acc(D) as acc:
                zeros = [(t.rearrange("(t p) c -> p t c", p=ET),
                          core.zeros[:, :].unsqueeze(1).to_broadcast([ET, NT + PADT, D])) for t in core.sums]
                edge_pass(core, Pass(f"gcn{i}", core.gcn_rows[i], D), win, acc, None, zeros if i == 0 else ())
                finish_narrow(core, f"fin4_{i}_{win}", acc, "gcn",
                              {"old": old[:, :, :], "new": g[:, :, :], "last": i == 1},
                              (core.gcn_rows[1].rearrange("(t p) c -> p t c", p=ET), g[:, :, :]) if i == 0 else None)

    with nc.sbuf_tensor(f"h_t5_{win}", [D, N], F32) as h_t:
        normalise(core, f"norm5_{win}", h_t)
        pair_tables(core, win, h_t)
    pair_pass(core, win)
    finish_pairs(core, win)


def store_rows(core, tag, table, rows):
    nc = core.nc
    with Stage(nc, tag) as st:
        stored = st.sem("stored")
        with nc.Block() as block:

            @block.sync
            def _(sp):
                sp.dma_start(table.rearrange("(t p) c -> p t c", p=ET), rows[:, :, :]).then_inc(stored, 16)
                sp.wait_ge(stored, 16)


def gnn_kernel(nc, a, out):
    with ExitStack() as ctx:
        core = Core(nc, ctx, a)
        prepare(core)
        prepare_weights(core)
        span = nc.values_load(core.span[0:1, 0:1], min_val=0, max_val=BE - 1)
        with nc.If(span < NARROW):
            nc.all_engine_barrier()
            layers(core, NARROW)
        with nc.Else():
            nc.all_engine_barrier()
            layers(core, FULL)
        store_rows(core, "out", out, core.x)


_WEIGHTS = ["L0_gnn_Wl1", "L0_gnn_Wr1", "L0_gnn_att1", "L0_gnn_b1", "L0_gnn_Wl2", "L0_gnn_Wr2", "L0_gnn_att2",
            "L0_gnn_b2", "L1_gnn_head_w", "L1_gnn_head_b", "L1_gnn_tail_w", "L1_gnn_tail_b", "L1_gnn_rel_w",
            "L3_gnn_pp_W", "L3_gnn_pp_b", "L3_gnn_pi_W1", "L3_gnn_pi_b1", "L3_gnn_pi_W2", "L3_gnn_ii_W", "L3_gnn_ii_b"]


def kernel(**inputs):
    import concourse.bacc as _bacc
    from concourse.bass_utils import run_bass_kernel_spmd as _run

    src = np.asarray(inputs["src"])
    src_t = np.zeros((P, TILES), src.dtype)
    src_t[0:ET] = src.reshape(TILES, ET).T
    arrays = {
        "x": inputs["x"], "src": src, "dst": inputs["dst"], "src_t": src_t,
        "dst_t": np.asarray(inputs["dst"]).reshape(TILES, ET).T,
        "next_t": np.roll(np.asarray(inputs["dst"]), -1).reshape(TILES, ET).T,
        "edge_type_t": np.asarray(inputs["edge_type_8"]).reshape(TILES, ET).T,
        "edge_weight_t": np.asarray(inputs["edge_weight"]).reshape(TILES, ET).T,
        "basis_t": np.asarray(inputs["edge_attr_8"]).reshape(TILES, ET, NBASIS).transpose(1, 0, 2).reshape(ET, -1),
    }
    for n in _WEIGHTS:
        arrays[n] = inputs[n]
    p = np.arange(P)
    arrays["ident"] = np.eye(P, dtype=np.float32)
    arrays["iota"] = p.astype(np.float32)
    arrays["iota_cols"] = np.stack([p, p // PARTS, N + p], 1).astype(np.float32)
    arrays["before"] = np.tril(np.ones((ET, ET), np.float32), -1)
    arrays["spare_rows"] = np.repeat((N + p).astype(np.int32)[:, None], RING * BT, 1)
    arrays["head_of"] = np.stack([[(p // D + 2 * c == h) for c in range(2)] for h in range(HEADS)]).astype(np.float32)
    nc = _bacc.Bacc("TRN2", target_bir_lowering=False, num_devices=1)
    arrays = {f"in_{n}": np.ascontiguousarray(v) for n, v in arrays.items()}
    a = {n[3:]: nc.dram_tensor(n, v.shape, mybir.dt.from_np(v.dtype), kind="ExternalInput").ap()
         for n, v in arrays.items()}
    out = nc.dram_tensor("out", (N, D), F32, kind="ExternalOutput").ap()
    gnn_kernel(nc, a, out)
    r = _run(nc, [arrays], core_ids=[0])
    return r.results[0]["out"]
```
